# Optimizing a Trainium2 kernel written in Bass

```python
import numpy as np
import jax
import jax.numpy as jnp

def _softmax(x, axis=-1):
    return jax.nn.softmax(x, axis=axis)

def _gelu(x):
    return jax.nn.gelu(x, approximate=True)

def _silu(x):
    return jax.nn.silu(x)

def _sigmoid(x):
    return jax.nn.sigmoid(x)

def _layernorm(x, axis=-1, eps=1e-05):
    m = jnp.mean(x, axis=axis, keepdims=True)
    v = jnp.var(x, axis=axis, keepdims=True)
    return (x - m) / jnp.sqrt(v + eps)

def _scatter_add(tgt, idx, src, axis=0):
    return tgt.at[idx].add(src)

def _segment_sum(src, seg, n):
    return jax.ops.segment_sum(src, seg, n)
kernel_name = 'mk_prb_d1_jaxref_r8_2a11e2'

def setup_inputs(seed: int=0):
    np.random.seed(seed)
    _w = jnp.asarray

    def _L0_attn_setup():
        import jax, jax.numpy as jnp
        import numpy as np
        NUM_HEADS = 16

        def _rope_tables(seq_len, head_dim, dtype):
            pos = jnp.arange(seq_len, dtype=jnp.float32)
            inv = jnp.power(10000.0, -2.0 * jnp.arange(head_dim // 2, dtype=jnp.float32) / head_dim)
            ang = pos[:, None] * inv[None, :]
            cos = jnp.repeat(jnp.cos(ang), 2, axis=-1).astype(dtype)
            sin = jnp.repeat(jnp.sin(ang), 2, axis=-1).astype(dtype)
            return (cos[None, None], sin[None, None])

        def _rotate_half_interleaved(x):
            x2 = jnp.stack([-x[..., 1::2], x[..., ::2]], axis=-1)
            return x2.reshape(x.shape)
        key = jax.random.key(seed)
        k0, k1, k2, k3 = jax.random.split(key, 4)
        B, N, C = (2, 256, 128)
        s = 1.0 / np.sqrt(C)
        return {'x': jax.random.normal(k0, (B, N, C), dtype=jnp.float32), 'Wq': jax.random.normal(k1, (C, C), dtype=jnp.float32) * s, 'Wk': jax.random.normal(k2, (C, C), dtype=jnp.float32) * s, 'Wv': jax.random.normal(k3, (C, C), dtype=jnp.float32) * s}
    _L0_attn_in = _L0_attn_setup()

    def _L0_ffn_setup():
        import jax, jax.numpy as jnp
        import numpy as np
        B, S, E, H, NE, TOP_K = (4, 256, 128, 256, 8, 2)
        key = jax.random.key(seed)
        ks = jax.random.split(key, 5)
        s = 0.02
        return {'x': jax.random.normal(ks[0], (B, S, E), jnp.float32), 'w1': jax.random.normal(ks[1], (NE, E, H), jnp.float32) * s, 'b1': jnp.zeros((NE, H), jnp.float32), 'w2': jax.random.normal(ks[2], (NE, H, H), jnp.float32) * s, 'b2': jnp.zeros((NE, H), jnp.float32), 'w3': jax.random.normal(ks[3], (NE, H, E), jnp.float32) * s, 'b3': jnp.zeros((NE, E), jnp.float32), 'gate_w': jax.random.normal(ks[4], (E, NE), jnp.float32) * s, 'gate_b': jnp.zeros((NE,), jnp.float32)}
    _L0_ffn_in = _L0_ffn_setup()
    _d = {'L0_attn_x': _L0_attn_in['x'], 'L0_attn_Wq': _L0_attn_in['Wq'], 'L0_attn_Wk': _L0_attn_in['Wk'], 'L0_attn_Wv': _L0_attn_in['Wv'], 'L0_ffn_w1': _L0_ffn_in['w1'], 'L0_ffn_b1': _L0_ffn_in['b1'], 'L0_ffn_w2': _L0_ffn_in['w2'], 'L0_ffn_b2': _L0_ffn_in['b2'], 'L0_ffn_w3': _L0_ffn_in['w3'], 'L0_ffn_b3': _L0_ffn_in['b3'], 'L0_ffn_gate_w': _L0_ffn_in['gate_w'], 'L0_ffn_gate_b': _L0_ffn_in['gate_b']}
    _x0 = _d['L0_attn_x']
    _d['L0_attn_x'] = jax.random.normal(jax.random.fold_in(jax.random.key(seed), 1), (4, 1024, 128), dtype=_x0.dtype)
    del _x0
    return _d

def reference(L0_attn_x, L0_attn_Wq, L0_attn_Wk, L0_attn_Wv, L0_ffn_w1, L0_ffn_b1, L0_ffn_w2, L0_ffn_b2, L0_ffn_w3, L0_ffn_b3, L0_ffn_gate_w, L0_ffn_gate_b):

    def _L0_attn_ref(x, Wq, Wk, Wv):
        import jax, jax.numpy as jnp
        import numpy as np
        NUM_HEADS = 16

        def _rope_tables(seq_len, head_dim, dtype):
            pos = jnp.arange(seq_len, dtype=jnp.float32)
            inv = jnp.power(10000.0, -2.0 * jnp.arange(head_dim // 2, dtype=jnp.float32) / head_dim)
            ang = pos[:, None] * inv[None, :]
            cos = jnp.repeat(jnp.cos(ang), 2, axis=-1).astype(dtype)
            sin = jnp.repeat(jnp.sin(ang), 2, axis=-1).astype(dtype)
            return (cos[None, None], sin[None, None])

        def _rotate_half_interleaved(x):
            x2 = jnp.stack([-x[..., 1::2], x[..., ::2]], axis=-1)
            return x2.reshape(x.shape)
        B, N, C = x.shape
        H = NUM_HEADS
        D = C // H
        scale = D ** (-0.5)

        def heads(y):
            return y.reshape(B, N, H, D).transpose(0, 2, 1, 3)
        q = heads(x @ Wq.T)
        k = heads(x @ Wk.T)
        v = heads(x @ Wv.T)
        cos, sin = _rope_tables(N, D, x.dtype)
        q = q * cos + _rotate_half_interleaved(q) * sin
        k = k * cos + _rotate_half_interleaved(k) * sin
        attn = jnp.einsum('bhnd,bhmd->bhnm', q, k) * scale
        attn = jax.nn.softmax(attn, axis=-1)
        out = jnp.einsum('bhnm,bhmd->bhnd', attn, v)
        return out.transpose(0, 2, 1, 3).reshape(B, N, C)

    def _L0_ffn_ref(x, w1, b1, w2, b2, w3, b3, gate_w, gate_b):
        import jax, jax.numpy as jnp
        import numpy as np
        B, S, E, H, NE, TOP_K = (4, 256, 128, 256, 8, 2)
        gate_weights = jax.nn.softmax(x @ gate_w + gate_b, axis=-1)
        topk_vals, topk_idx = jax.lax.top_k(gate_weights, TOP_K)
        h = jax.nn.gelu(jnp.einsum('bse,neh->bsnh', x, w1) + b1, approximate=False)
        h = jax.nn.gelu(jnp.einsum('bsnh,nhk->bsnk', h, w2) + b2, approximate=False)
        expert_out = jnp.einsum('bsnh,nhe->bsne', h, w3) + b3
        gathered = jnp.take_along_axis(expert_out, topk_idx[..., None], axis=2)
        return jnp.sum(topk_vals[..., None] * gathered, axis=2)
    x = L0_attn_x
    xn = _layernorm(x, axis=-1)
    x = x + _L0_attn_ref(xn, L0_attn_Wq, L0_attn_Wk, L0_attn_Wv) + _L0_ffn_ref(xn, L0_ffn_w1, L0_ffn_b1, L0_ffn_w2, L0_ffn_b2, L0_ffn_w3, L0_ffn_b3, L0_ffn_gate_w, L0_ffn_gate_b)
    return x

_drawn_inputs = setup_inputs


def setup_inputs(seed=0):
    import zlib

    import numpy as np

    out = dict(_drawn_inputs(seed))
    spreads = {'L0_ffn_b1': (0.0, 0.8),
     'L0_ffn_b2': (0.0, 0.8),
     'L0_ffn_b3': (0.0, 0.333),
     'L0_ffn_gate_b': (0.0, 0.47)}
    factors = {'L0_ffn_w1': 8.0, 'L0_ffn_w2': 8.0, 'L0_ffn_w3': 8.0, 'L0_ffn_gate_w': 2.893}
    for name, (base, spread) in spreads.items():
        noise = np.random.default_rng([zlib.crc32(name.encode()), seed]).standard_normal(out[name].shape)
        drawn = base * np.exp(spread * noise) if base else spread * noise
        out[name] = jnp.asarray(drawn.astype(out[name].dtype))
    for name, factor in factors.items():
        out[name] = (out[name] * factor).astype(out[name].dtype)
    return out
```

```python
import concourse.bass as bass
from concourse import mybir
from contextlib import ExitStack

F32 = mybir.dt.float32
F32R = mybir.dt.float32r
I32 = mybir.dt.int32
U32 = mybir.dt.uint32
ACT = mybir.ActivationFunctionType
ALU = mybir.AluOpType
AX = mybir.AxisListType

P = 128
B, N, C = 4, 1024, 128
H, D = 16, 8
HG = 4
G = H // HG
STEPS = B * G
TILES = B * N // P
BT = N // P
HALF = N // 2
MT = N // P
SCALE = float(D) ** -0.5
EPS = 1e-5
E_, HID = 8, 256
ST = 256
SLOT_TILES = (2 * B * N + E_ * (ST - 1)) // ST
SLOT_ROOM = SLOT_TILES + 1
UNITS = 2 * MT * 2
BLOCKS = 2 * MT
SCORE_RING = 3
PROB_RING = 4
SPLIT = 8
SAFE_SCORE = 60.0


def build(nc, x, Wq, Wk, Wv, w1, b1, w2, b2, w3, b3, gw, gb, rope_cos, rope_sin, consts, out):
    ctx = ExitStack()
    with ctx:
        def sb(name, shape, dt=F32):
            return ctx.enter_context(nc.sbuf_tensor(name, shape, dt))

        def sem(name):
            return ctx.enter_context(nc.semaphore(name))

        def dram(name, shape, dt=F32):
            return nc.dram_tensor(name, shape, dt, kind="Internal").ap()

        qhi_d, qlo_d, khi_d, klo_d = (dram(n, (B * C, N)) for n in ("qhi_d", "qlo_d", "khi_d", "klo_d"))
        shift_d = dram("shift_d", (STEPS, 2, HG, N))
        slots_x_d = dram("slots_x_d", (SLOT_ROOM * ST, C))
        slots_y_d = dram("slots_y_d", (SLOT_TILES * ST, C))

        x_all = sb("x_all", [P, TILES, C])
        xn_all = sb("xn_all", [P, TILES, C])
        v_all = sb("v_all", [P, STEPS, MT, HG * D])
        attn_all = sb("attn_all", [P, STEPS, BT, HG * D])
        cst = sb("cst", [P, 3 * P + 8 + 40 + 32 + H])
        ident, before, ones = cst[:, 0:P], cst[:, P:2 * P], cst[:, 2 * P:3 * P]
        prefer = cst[:, 384:392]
        iota_tile = cst[:, 392:432]
        iota_fill = cst[:, 432:464]
        head_of = cst[:, 464:480]

        k_st = sb("k_st", [P, N], F32R)
        q_mv = sb("q_mv", [P, HG, N], F32R)
        v_st = sb("v_st", [P, MT, HG, 32])
        probs = sb("probs", [P, PROB_RING, HG, HALF])
        o_sb = sb("o_sb", [P, 2, HALF])
        o_rec = sb("o_rec", [P, 4 * HG])

        logits = sb("logits", [P, TILES, E_])
        gates = sb("gates", [P, TILES, 2])
        slot_i = sb("slot_i", [P, 2, TILES], I32)
        expert_i = sb("expert_i", [P, 40], I32)
        gbias = sb("gbias", [P, E_])
        gw_sb = sb("gw_sb", [P, E_])
        b_raw = sb("b_raw", [4 * E_, P])
        b12 = sb("b12", [P, 2, E_, 2])
        b1_sb, b2_sb = b12[:, 0], b12[:, 1]
        b3_sb = sb("b3_sb", [P, E_, C])
        gath = sb("gath", [P, 8, C])

        pr = probs[:].rearrange("p r h n -> p (r h n)")
        cos_sb, sin_sb = pr[:, 0:1024], pr[:, 1024:2048]
        xnb = pr[:, 2048:3072].rearrange("p (k c) -> p k c", c=C)
        xnT = pr[:, 3072:4096]
        t_cos, t_sin = pr[:, 4096:4608], pr[:, 4608:5120]
        rot = pr[:, 5120:6144].rearrange("p (u n) -> p u n", u=2)
        w_raw = pr[:, 6144:6528]
        zeros = sb("zeros", [P, 1024])
        wT = sb("wT", [P, 5, C])
        part_hi = sb("part_hi", [P, 2, HALF], F32R)
        part_lo = sb("part_lo", [P, 2, HALF], F32R)
        stats = sb("stats", [P, TILES, 6])
        mean = sb("mean", [P, TILES])
        std = sb("std", [P, 4, TILES])
        peak = sb("peak", [H, 2, 2 * B])
        squares = sb("squares", [P, 2, HALF], F32R)
        head_r = sb("head_r", [P, H], F32R)
        bound = sb("bound", [H, 3])
        bound_row = sb("bound_row", [1, 2])
        flag_i = sb("flag_i", [1, 1], I32)
        row_max = sb("row_max", [P, MT, HG])
        shift_hi = sb("shift_hi", [P, MT, HG], F32R)
        shift_nt = sb("shift_nt", [P, 2 * MT, 2, HG])
        shift_rows = sb("shift_rows", [P, P])
        rt = sb("rt", [P, 12, TILES, E_])
        rs = sb("rs", [P, 8, TILES])
        rcmp = sb("rcmp", [P, 40, E_])
        r8 = sb("r8", [P, 4, E_])

        w1_sb = sb("w1_sb", [P, 2, HID])
        w2_sb = sb("w2_sb", [P, 2, 2, HID])
        w3_sb = sb("w3_sb", [P, 2, 2, C])
        xs_sb = sb("xs_sb", [P, 2, 2, C])
        xsT = sb("xsT", [P, 2, ST])
        h1 = sb("h1", [P, 2, 2, ST])
        h2 = sb("h2", [P, 2, 2, ST])
        y_sb = sb("y_sb", [P, 2, 2, C])

        ps = ctx.enter_context(nc.psum_tensor("ps", [P, 4096], F32))

        def bank(k, n=1):
            return ps[:, 512 * k:512 * (k + n)]

        trans_ps, v_ps = bank(0, 2), bank(6, 2)
        proj_ps = [bank(2, 2), bank(4, 2)]
        score_ps = [bank(2 * k, 2) for k in range(SCORE_RING)]
        o_ps = [bank(6), bank(7)]
        xs_ps, h1_ps = [bank(0), bank(1)], [bank(2), bank(3)]
        h2_ps, y_ps = [bank(4), bank(5)], [bank(6), bank(7)]

        names = """x_loaded0 x_loaded1 x_loaded2 x_loaded3 small_loaded weights_loaded bias_loaded
            wT_made wT_copied stats_made std_made std_fixed xnb_made xnb_saved xnT_made_v xnT_made_a
            trans_done proj_done proj_read rot_made hi_made lo_made parts_stored0 parts_stored1
            v_done v_copied gate_done gate_copied dve_chain dve_pro_chain
            max_made exp_made masks_made prefix_made routed zero_made x_zeroed x_scattered
            st_init ka_loaded kb_loaded q0_loaded q1_loaded v_loaded scores_done exp_done pv_done
            o_copied o_turned o_free norm_chain
            w1_in0 w1_in1 w2_in0 w2_in1 w3_in0 w3_in1 xs_in0 xs_in1 xs_turned xsT_made
            l1_done l2_done l3_done g1_done g2_done y_made y_stored0 y_stored1
            squares_made norms_done norms_read bound_made bound_summed flag_made shift_zeroed mx_loaded mx_scores mx_read mx_made mx_turned mx_copied mx_stored
            gathered combined comb_chain out_ready out_stored attn_ended experts_ended""".split()
        S = {n: sem(n) for n in names}
        parts_stored = [S["parts_stored0"], S["parts_stored1"]]
        w1_in, w2_in, w3_in, xs_in, y_stored = ([S[f"{n}{k}"] for k in range(2)]
                                                for n in ("w1_in", "w2_in", "w3_in", "xs_in", "y_stored"))
        QK_LOADS = 3
        Q_LOADS = 3 * HG + 1

        block = ctx.enter_context(nc.Block())

        @block.sync
        def _(sp):
            sp.sem_inc(S["parts_stored0"], 32)
            sp.sem_inc(S["parts_stored1"], 32)
            sp.sem_inc(S["xnb_saved"], 16)
            xv = x.rearrange("b (k p) c -> p b k c", p=P)
            sp.dma_start(x_all[:, 0:BT, :], xv[:, 0]).then_inc(S["x_loaded0"], 16)
            for k, w in enumerate((Wq, Wk, Wv)):
                sp.dma_start(w_raw[:, k * C:(k + 1) * C], w).then_inc(S["small_loaded"], 16)
            sp.dma_start(cst[:], consts).then_inc(S["small_loaded"], 16)
            for k, bias in enumerate((b1, b2)):
                sp.dma_start(b_raw[2 * E_ * k:2 * E_ * (k + 1), :], bias.rearrange("e (h p) -> (e h) p", p=P))\
                    .then_inc(S["small_loaded"], 16)
            for b in range(1, B):
                sp.dma_start(x_all[:, b * BT:(b + 1) * BT, :], xv[:, b]).then_inc(S[f"x_loaded{b}"], 16)
            sp.dma_start(cos_sb, rope_cos).then_inc(S["weights_loaded"], 16)
            sp.dma_start(sin_sb, rope_sin).then_inc(S["weights_loaded"], 16)
            sp.dma_start(gw_sb[:], gw).then_inc(S["weights_loaded"], 16)
            sp.dma_start(gbias[:], gb.rearrange("(a e) -> a e", a=1).partition_broadcast(P)).then_inc(S["weights_loaded"], 16)
            sp.dma_start(b3_sb[:].rearrange("p e c -> p (e c)"),
                         b3.rearrange("(a e) c -> a (e c)", a=1).partition_broadcast(P)).then_inc(S["bias_loaded"], 16)
            sp.wait_ge(S["zero_made"], 1)
            for r in range(SLOT_ROOM // 4):
                sp.dma_start(slots_x_d[r * 4 * ST:(r + 1) * 4 * ST, :].rearrange("(p j) c -> p (j c)", p=P),
                             zeros[:]).then_inc(S["x_zeroed"], 16)

            sp.dma_start(shift_d.rearrange("t a h (c n) -> (t a h) c n", n=N),
                         zeros[:].rearrange("p (c n) -> p c n", n=N)).then_inc(S["shift_zeroed"], 16)

            with sp.Fori(0, B) as b:
                sp.wait_ge(S["xnb_made"], b * 1 + 1)
                sp.dma_start(xn_all[:, bass.ds(b * BT, BT), :], xnb).then_inc(S["xnb_saved"], 16)
                for half in range(2):
                    for u, (hi_d, lo_d) in enumerate(((qhi_d, qlo_d), (khi_d, klo_d))):
                        sp.wait_ge(S["lo_made"], b * 4 + (2 * half + u + 3))
                        for d, s in ((hi_d, part_hi), (lo_d, part_lo)):
                            sp.dma_start(d[bass.ds(b * C, C), half * HALF:(half + 1) * HALF],
                                         s[:, u, :].bitcast(F32)).then_inc(parts_stored[u], 16)
            for u in range(2):
                sp.wait_ge(parts_stored[u], 32 + 16 * 4 * B)

            def load_k(t, part, signal):
                cols = slice(part * HALF, (part + 1) * HALF)
                for strip, src in enumerate((khi_d, klo_d, khi_d)):
                    sp.dma_start(k_st[32 * strip:32 * strip + 32, cols].bitcast(F32),
                                 src[bass.ds(t * 32, 32), cols]).then_inc(signal, 16)

            def load_q(t, half, signal):
                cols = slice(half * HALF, (half + 1) * HALF)
                for strip, src in enumerate((qhi_d, qhi_d, qlo_d)):
                    for h in range(HG):
                        r = 32 * strip + D * h
                        sp.dma_start(q_mv[r:r + D, h, cols].bitcast(F32),
                                     src[bass.ds(t * 32 + D * h, D), cols]).then_inc(signal, 16)

            def load_shift(t, half, signal):
                cols = slice(half * HALF, (half + 1) * HALF)
                sp.dma_start(q_mv[3 * 32:3 * 32 + 2, :, cols].bitcast(F32),
                             shift_d[bass.ds(t, 1), :, :, cols].rearrange("t a h n -> (t a) h n")).then_inc(signal, 16)

            sp.wait_ge(S["st_init"], 1)
            sp.wait_ge(S["shift_zeroed"], 16)
            sp.wait_ge(S["flag_made"], 1)
            with sp.If(sp.value_load(flag_i[0:1, 0:1], min_val=0, max_val=1)):
                with sp.Fori(0, STEPS) as t:
                    sp.wait_ge(S["mx_scores"], t * (HG * MT) + 1)
                    for part in range(2):
                        load_k(t, part, S["mx_loaded"])
                        load_q(t, part, S["mx_loaded"])
                sp.wait_ge(S["mx_stored"], 16 * MT * (STEPS + 1))
            load_q(0, 0, S["q0_loaded"])
            load_shift(0, 0, S["q0_loaded"])
            load_k(0, 0, S["ka_loaded"])
            load_k(0, 1, S["kb_loaded"])
            load_q(0, 1, S["q1_loaded"])
            load_shift(0, 1, S["q1_loaded"])

            def attention_loads(lo, hi):
                with sp.Fori(lo, hi) as t:
                    sp.wait_ge(S["scores_done"], t * UNITS + UNITS // 2)
                    load_q(t + 1, 0, S["q0_loaded"])
                    load_shift(t + 1, 0, S["q0_loaded"])
                    sp.wait_ge(S["scores_done"], t * UNITS + 3 * UNITS // 4)
                    load_k(t + 1, 0, S["ka_loaded"])
                    sp.wait_ge(S["scores_done"], t * UNITS + UNITS)
                    load_k(t + 1, 1, S["kb_loaded"])
                    load_q(t + 1, 1, S["q1_loaded"])
                    load_shift(t + 1, 1, S["q1_loaded"])

            attention_loads(0, SPLIT)

            sp.wait_ge(S["x_scattered"], 16 * 2 * TILES)
            sp.wait_ge(S["routed"], 2)

            def load_tile(j, par, first):
                e = sp.value_load(expert_i[0:1, bass.ds(j, 1)], min_val=0, max_val=E_ - 1)
                if not first:
                    sp.wait_ge(S["xs_turned"], j - 1)
                sp.dma_start(xs_sb[:, par], slots_x_d[bass.ds(j * ST, ST), :].rearrange("(k p) c -> p k c", p=P)).then_inc(xs_in[par], 16)
                if not first:
                    sp.wait_ge(S["l1_done"], j - 1)
                sp.dma_start(w1_sb[:, par], w1[bass.ds(e, 1)].rearrange("a p n -> p (a n)")).then_inc(w1_in[par], 16)
                if not first:
                    sp.wait_ge(S["l2_done"], j - 1)
                sp.dma_start(w2_sb[:, par], w2[bass.ds(e, 1)].rearrange("a (k p) n -> p (a k) n", p=P)).then_inc(w2_in[par], 16)
                if not first:
                    sp.wait_ge(S["l3_done"], j - 1)
                sp.dma_start(w3_sb[:, par], w3[bass.ds(e, 1)].rearrange("a (k p) n -> p (a k) n", p=P)).then_inc(w3_in[par], 16)

            load_tile(0, 0, True)
            load_tile(1, 1, True)
            with sp.Fori(0, (SLOT_TILES - 1) // 2) as i:
                load_tile(i * 2 + 2, 0, False)
                load_tile(i * 2 + 3, 1, False)

            attention_loads(SPLIT, STEPS - 1)

            ov = out.rearrange("b (k p) c -> p b k c", p=P)
            for b in range(B):
                sp.wait_ge(S["out_ready"], b + 1)
                sp.dma_start(ov[:, b], x_all[:, b * BT:(b + 1) * BT, :]).then_inc(S["out_stored"], 16)
            sp.wait_ge(S["out_stored"], 16 * B)

        @block.gpsimd
        def _(pool):
            pool.sem_inc(S["lo_made"], 2)
            nc.gpsimd.memset(zeros[:], 0.0).then_inc(S["zero_made"], 1)
            with pool.Fori(0, B) as b:
                for n in range(4):
                    u, m = n % 2, n // 2
                    pool.wait_ge(S["hi_made"], b * 4 + (n + 1))
                    pool.wait_ge(parts_stored[u], b * 64 + 32 * (m + 1))
                    nc.gpsimd.tensor_tensor(part_lo[:, u, :], rot[:, u, :], part_hi[:, u, :].bitcast(F32),
                                            ALU.subtract).then_inc(S["lo_made"], 1)
            pool.wait_ge(S["x_zeroed"], 16 * (SLOT_ROOM // 4))
            pool.wait_ge(S["xnb_saved"], 16 + 16 * B)
            pool.wait_ge(S["routed"], 2)
            for i in range(TILES):
                for c in range(2):
                    nc.gpsimd.indirect_dma_start(
                        out=slots_x_d, out_offset=bass.IndirectOffsetOnAxis(ap=slot_i[:, c, i:i + 1].bitcast(U32), axis=0),
                        in_=xn_all[:, i, :], in_offset=None).then_inc(S["x_scattered"], 16)
            def store_y(j, par):
                pool.wait_ge(S["y_made"], j + 3)
                pool.dma_start(slots_y_d[bass.ds(j * ST, ST), :].rearrange("(k p) c -> p k c", p=P),
                               y_sb[:, par]).then_inc(y_stored[par], 16)

            with pool.Fori(0, (SLOT_TILES - 1) // 2) as i:
                store_y(i * 2, 0)
                store_y(i * 2 + 1, 1)
            store_y(SLOT_TILES - 1, 0)
            pool.wait_ge(y_stored[0], 16 * ((SLOT_TILES + 1) // 2))
            pool.wait_ge(y_stored[1], 16 * (SLOT_TILES // 2))
            for i in range(TILES // 4):
                if i >= 1:
                    pool.wait_ge(S["combined"], i)
                for c in range(2):
                    for k in range(4):
                        nc.gpsimd.indirect_dma_start(
                            out=gath[:, 4 * c + k, :], out_offset=None, in_=slots_y_d,
                            in_offset=bass.IndirectOffsetOnAxis(ap=slot_i[:, c, 4 * i + k:4 * i + k + 1].bitcast(U32), axis=0))\
                            .then_inc(S["gathered"], 16)

        @block.scalar
        def _(act):
            act.sem_inc(S["v_copied"], 1)
            act.sem_inc(S["squares_made"], 2)
            act.wait_ge(S["stats_made"], 1)
            nc.scalar.activation(std[:, 0, :], std[:, 1, :], ACT.Sqrt).then_inc(S["std_made"], 1)
            act.wait_ge(S["std_fixed"], 1)
            with act.Fori(0, B) as b:
                act.wait_ge(S["trans_done"], b * 2 + 2)
                act.wait_ge(S["xnb_saved"], b * 16 + 16)
                for k in range(BT):
                    ins = nc.scalar.activation(xnb[:, k, :], x_all[:, bass.ds(b * BT + k, 1), :].rearrange("p a c -> p (a c)"),
                                               ACT.Identity, bias=std[:, 3, bass.ds(b * BT + k, 1)],
                                               scale=std[:, 2, bass.ds(b * BT + k, 1)])
                ins.then_inc(S["xnb_made"], 1)
                act.wait_ge(S["trans_done"], b * 2 + 4)
                nc.scalar.activation(xnT[:, HALF:N], trans_ps[:, HALF:N], ACT.Copy).then_inc(S["xnT_made_a"], 1)
                act.wait_ge(S["v_done"], b * 1 + 1)
                nc.scalar.activation(v_all[:, bass.ds(b * G, G), :, :].rearrange("p g m c -> p m g c"),
                                     v_ps.rearrange("p (m g c) -> p m g c", g=G, c=HG * D), ACT.Copy).then_inc(S["v_copied"], 1)
                for n in range(4):
                    u, m = n % 2, n // 2
                    act.wait_ge(S["rot_made"], b * 4 + (n + 1))
                    act.wait_ge(parts_stored[u], b * 64 + 32 * (m + 1))
                    nc.scalar.activation(part_hi[:, u, :], rot[:, u, :], ACT.Copy).then_inc(S["hi_made"], 1)
                    act.wait_ge(S["norms_done"], b * 4 + (n + 1))
                    nc.scalar.activation(squares[:, u, :], rot[:, u, :], ACT.Square).then_inc(S["squares_made"], 1)
            act.sem_inc(S["mx_stored"], 16 * MT)
            act.wait_ge(S["shift_zeroed"], 16)
            act.wait_ge(S["flag_made"], 1)
            act.wait_ge(S["max_made"], 1)
            nc.scalar.activation(rt[:, 1], rt[:, 0], ACT.Exp).then_inc(S["exp_made"], 1)

            with act.If(act.value_load(flag_i[0:1, 0:1], min_val=0, max_val=1)):
                with act.Fori(0, STEPS) as t:
                    act.wait_ge(S["mx_copied"], t + 1)
                    for nt in range(MT):
                        act.dma_start(shift_d[bass.ds(t, 1), :, :, nt * P:(nt + 1) * P].rearrange("t a h n -> (t a h) n"),
                                      shift_rows[nt * 2 * HG:(nt + 1) * 2 * HG, :]).then_inc(S["mx_stored"], 16)

            def attention_exps(t):
                for u in range(UNITS):
                    j, pair = divmod(u, 2)
                    act.wait_ge(S["scores_done"], t * UNITS + (u + 1))
                    if pair == 0:
                        act.wait_ge(S["pv_done"], t * BLOCKS + (BLOCKS + j + 1 - PROB_RING))
                    nc.scalar.activation(probs[:, j % PROB_RING, 2 * pair:2 * pair + 2, :],
                                         score_ps[u % SCORE_RING].rearrange("p (h n) -> p h n", h=2),
                                         ACT.Exp, scale=SCALE).then_inc(S["exp_done"], 1)

            with act.Fori(0, SPLIT) as t:
                attention_exps(t)

            def gelus(j, par):
                e = act.value_load(expert_i[0:1, bass.ds(j, 1)], min_val=0, max_val=E_ - 1)
                for ready, signal, src, dst, bias in (("l1_done", "g1_done", h1_ps, h1, b1_sb), ("l2_done", "g2_done", h2_ps, h2, b2_sb)):
                    act.wait_ge(S[ready], j + 1)
                    for k in range(2):
                        ins = nc.scalar.activation(dst[:, par, k, :], src[par][:, k * ST:(k + 1) * ST], ACT.Gelu,
                                                   bias=bias[:, bass.ds(e, 1), k])
                    ins.then_inc(S[signal], 1)

            act.wait_ge(S["routed"], 2)
            act.wait_ge(S["wT_copied"], 1)
            gelus(0, 0)
            with act.Fori(0, (SLOT_TILES - 1) // 2) as i:
                gelus(i * 2 + 1, 1)
                gelus(i * 2 + 2, 0)
            with act.Fori(SPLIT, STEPS) as t:
                attention_exps(t)

        @block.vector
        def _(dve):
            links = {}

            def link(ins, chain="dve_chain", base=None):
                links[chain] = links.get(chain, 0) + 1
                ins.then_inc(S[chain], 1)
                dve.wait_ge(S[chain], links[chain] if base is None else base + links[chain])

            dve.sem_inc(S["proj_read"], 2)
            dve.sem_inc(S["mx_read"], 2)
            dve.sem_inc(S["norms_read"], 1)
            dve.sem_inc(S["gate_copied"], 1)
            dve.sem_inc(S["o_free"], 2)
            dve.sem_inc(S["y_made"], 2)
            for b in range(B):
                dve.wait_ge(S[f"x_loaded{b}"], 16)
                with dve.Fori(b * BT, (b + 1) * BT) as k:
                    ins = nc.vector.bn_stats(stats[:, bass.ds(k, 1), :].rearrange("p a c -> p (a c)"),
                                             x_all[:, bass.ds(k, 1), :].rearrange("p a c -> p (a c)"))
                    ins.then_inc(S["dve_pro_chain"], 1)
            dve.wait_ge(S["dve_pro_chain"], TILES)
            link(nc.vector.tensor_tensor(std[:, 0, :], stats[:, :, 1], stats[:, :, 4], ALU.add))
            nc.vector.tensor_scalar(mean[:], std[:, 0, :], 0.5, None, ALU.mult)
            link(nc.vector.tensor_tensor(std[:, 1, :], stats[:, :, 1], stats[:, :, 4], ALU.subtract))
            link(nc.vector.scalar_tensor_tensor(std[:, 2, :], std[:, 1, :], 0.25, std[:, 1, :], ALU.mult, ALU.mult))
            link(nc.vector.tensor_tensor(std[:, 3, :], stats[:, :, 2], stats[:, :, 5], ALU.add))
            link(nc.vector.scalar_tensor_tensor(std[:, 0, :], std[:, 3, :], 1.0 / C, std[:, 2, :], ALU.mult, ALU.add))
            nc.vector.tensor_scalar(std[:, 1, :], std[:, 0, :], EPS, None, ALU.add).then_inc(S["stats_made"], 1)
            dve.wait_ge(S["wT_made"], 1)
            for k in range(3):
                src = v_ps[:, k * C:(k + 1) * C]
                ins = nc.vector.tensor_copy(wT[:, 2 * k, :], src)
                if k < 2:
                    for o in range(2):
                        ins = nc.vector.tensor_copy(wT[:, 2 * k + 1, o::2], src[:, 1 - o::2])
            ins = nc.vector.tensor_copy(b12[:].rearrange("p l e h -> p (l e h)"), v_ps[:, 3 * C:3 * C + 4 * E_])
            ins = nc.vector.tensor_copy(head_r[:], head_of)
            ins.then_inc(S["wT_copied"], 1)
            dve.wait_ge(S["std_made"], 1)
            link(nc.vector.reciprocal(std[:, 2, :], std[:, 0, :]))
            link(nc.vector.tensor_tensor(std[:, 3, :], std[:, 1, :], std[:, 2, :], ALU.mult))
            link(nc.vector.tensor_tensor(std[:, 2, :], std[:, 3, :], std[:, 0, :], ALU.add))
            link(nc.vector.tensor_scalar(std[:, 3, :], std[:, 2, :], 0.5, None, ALU.mult))
            link(nc.vector.reciprocal(std[:, 2, :], std[:, 3, :]))
            nc.vector.scalar_tensor_tensor(std[:, 3, :], mean[:], -1.0, std[:, 2, :], ALU.mult, ALU.mult)\
                .then_inc(S["std_fixed"], 1)
            nc.vector.memset(shift_nt[:], 0.0)
            nc.vector.memset(q_mv[:].bitcast(F32), 0.0)
            nc.vector.memset(k_st[96:128, :].bitcast(F32), 1.0)
            link(nc.vector.memset(v_st[:], 0.0))
            nc.vector.memset(v_st[:, :, :, D:D + 1], 1.0).then_inc(S["st_init"], 1)
            dve.wait_ge(S["weights_loaded"], 64)

            def norm_peak(b, n):
                dve.wait_ge(S["norms_done"], b * 4 + (n + 3))
                nc.vector.tensor_reduce(peak[:, n % 2, bass.ds(b * 2 + n // 2, 1)], trans_ps[0:H, HALF:N], AX.X, ALU.max)\
                    .then_inc(S["norms_read"], 1)

            with dve.Fori(0, B) as b:
                dve.wait_ge(S["trans_done"], b * 2 + 3)
                nc.vector.tensor_copy(xnT[:, 0:HALF], trans_ps[:, 0:HALF]).then_inc(S["xnT_made_v"], 1)
                for n in range(4):
                    u, m = n % 2, n // 2
                    dve.wait_ge(S["proj_done"], b * 4 + (n + 1))
                    cols = slice(m * HALF, (m + 1) * HALF)
                    nc.vector.tensor_tensor(t_cos, proj_ps[u][:, 0:HALF], cos_sb[:, cols], ALU.mult)
                    ins = nc.vector.tensor_tensor(t_sin, proj_ps[u][:, HALF:N], sin_sb[:, cols], ALU.mult)
                    ins.then_inc(S["proj_read"], 1)
                    dve.wait_ge(S["proj_read"], b * 4 + (n + 3))
                    dve.wait_ge(S["lo_made"], b * 4 + (n + 1))
                    dve.wait_ge(S["squares_made"], b * 4 + (n + 1))
                    nc.vector.tensor_tensor(rot[:, u, :], t_cos, t_sin, ALU.add).then_inc(S["rot_made"], 1)
                    dve.wait_ge(S["rot_made"], b * 4 + (n + 1))
                    if n >= 1:
                        norm_peak(b, n - 1)
                dve.wait_ge(S["gate_done"], b * 1 + 1)
                nc.vector.tensor_tensor(logits[:, bass.ds(b * BT, BT), :],
                                        trans_ps[:, 0:BT * E_].rearrange("p (k e) -> p k e", e=E_),
                                        gbias[:].rearrange("p (a e) -> p a e", a=1).to_broadcast([P, BT, E_]), ALU.add).then_inc(S["gate_copied"], 1)
                norm_peak(b, 3)
            dve.wait_ge(S["gate_copied"], B + 1)

            dve.wait_ge(S["norms_read"], 4 * B + 1)
            link(nc.vector.tensor_reduce(bound[:, 0:2], peak[:], AX.X, ALU.max))
            nc.vector.tensor_tensor(bound[:, 2:3], bound[:, 0:1], bound[:, 1:2], ALU.mult).then_inc(S["bound_made"], 1)
            dve.wait_ge(S["bound_summed"], 1)
            link(nc.vector.tensor_reduce(bound_row[:, 0:1], trans_ps[0:1, 512:512 + H], AX.X, ALU.max))
            link(nc.vector.tensor_scalar(bound_row[:, 1:2], bound_row[:, 0:1], (SAFE_SCORE / SCALE) ** 2, None, ALU.is_le))
            nc.vector.tensor_scalar(flag_i[:], bound_row[:, 1:2], -1.0, 1.0, ALU.mult, ALU.add).then_inc(S["flag_made"], 1)

            def per_tile(a):
                return a.rearrange("p (k a) -> p k a", a=1).to_broadcast([P, TILES, E_])

            link(nc.vector.tensor_reduce(rs[:, 0], logits[:], AX.X, ALU.max))
            nc.vector.tensor_tensor(rt[:, 0], logits[:], per_tile(rs[:, 0]), ALU.subtract).then_inc(S["max_made"], 1)
            dve.wait_ge(S["exp_made"], 1)
            link(nc.vector.tensor_reduce(rs[:, 1], rt[:, 1], AX.X, ALU.add))
            link(nc.vector.reciprocal(rs[:, 2], rs[:, 1]))
            link(nc.vector.tensor_tensor(rt[:, 2], rt[:, 1], per_tile(rs[:, 2]), ALU.mult))
            prefer_b = prefer.rearrange("p (a e) -> p a e", a=1).to_broadcast([P, TILES, E_])
            for c in range(2):
                src, one = rt[:, 2 + c], rt[:, 4 + c]
                link(nc.vector.tensor_reduce(gates[:, :, c], src, AX.X, ALU.max))
                link(nc.vector.tensor_tensor(rt[:, 6], src, per_tile(gates[:, :, c]), ALU.is_equal))
                link(nc.vector.tensor_tensor(rt[:, 7], rt[:, 6], prefer_b, ALU.mult))
                link(nc.vector.tensor_reduce(rs[:, 3], rt[:, 7], AX.X, ALU.max))
                link(nc.vector.tensor_tensor(one, rt[:, 7], per_tile(rs[:, 3]), ALU.is_equal))
                if c == 0:
                    link(nc.vector.scalar_tensor_tensor(rt[:, 3], one, -2.0, src, ALU.mult, ALU.add))
            nc.vector.tensor_tensor(rt[:, 8], rt[:, 4], rt[:, 5], ALU.add).then_inc(S["masks_made"], 1)
            dve.wait_ge(S["prefix_made"], 1)
            pre = v_ps[:, 0:TILES * E_].rearrange("p (k e) -> p k e", e=E_)
            tot = v_ps[:, 512:512 + TILES * E_].rearrange("p (k e) -> p k e", e=E_)
            link(nc.vector.tensor_copy(rt[:, 9], tot))
            nc.vector.memset(rt[:, 7], 1.0)
            link(nc.vector.memset(rcmp[:], 1.0))
            for e in range(E_):
                ins = nc.vector.tensor_tensor_scan(rt[:, 10, :, e], rt[:, 7, :, e], rt[:, 9, :, e], 0.0, ALU.mult, ALU.add)
            link(ins)
            fill_b = iota_fill.rearrange("p (k a) -> p k a", a=1).to_broadcast([P, TILES, E_])
            count_b = rt[:, 10, TILES - 1:TILES, :].to_broadcast([P, TILES, E_])
            link(nc.vector.tensor_tensor(rt[:, 6], count_b, fill_b, ALU.is_gt))
            link(nc.vector.tensor_reduce(r8[:, 0], rt[:, 6].rearrange("p k e -> p e k"), AX.X, ALU.add))
            link(nc.vector.tensor_tensor_scan(r8[:, 1], rcmp[:, 0, :], r8[:, 0], 0.0, ALU.mult, ALU.add))
            link(nc.vector.tensor_tensor(r8[:, 2], r8[:, 1], r8[:, 0], ALU.subtract))
            link(nc.vector.tensor_scalar(r8[:, 3], r8[:, 2], float(ST), None, ALU.mult))
            link(nc.vector.tensor_tensor(rt[:, 6], rt[:, 10], rt[:, 9], ALU.subtract))
            link(nc.vector.tensor_tensor(rt[:, 7], rt[:, 6], pre, ALU.add))
            link(nc.vector.tensor_tensor(rt[:, 6], rt[:, 7], r8[:, 3:4].to_broadcast([P, TILES, E_]), ALU.add))
            for c in range(2):
                link(nc.vector.tensor_tensor(rt[:, 7], rt[:, 4 + c], rt[:, 6], ALU.mult))
                link(nc.vector.tensor_reduce(rs[:, 4 + c], rt[:, 7], AX.X, ALU.add))
            nc.vector.tensor_copy(slot_i[:], rs[:, 4:6]).then_inc(S["routed"], 1)
            link(nc.vector.tensor_tensor(rcmp[:], r8[:, 1:2].to_broadcast([P, 40, E_]),
                                         iota_tile.rearrange("p (k a) -> p k a", a=1).to_broadcast([P, 40, E_]), ALU.is_le))
            link(nc.vector.tensor_reduce(rt[:, 0].rearrange("p k e -> p (k e)")[:, 0:40], rcmp[:], AX.X, ALU.add))
            nc.vector.tensor_scalar(expert_i[:], rt[:, 0].rearrange("p k e -> p (k e)")[:, 0:40], float(E_ - 1), None, ALU.min)\
                .then_inc(S["routed"], 1)
            dve.wait_ge(S["routed"], 2)

            with dve.If(dve.value_load(flag_i[0:1, 0:1], min_val=0, max_val=1)):
                with dve.Fori(0, STEPS) as t:
                    for h in range(HG):
                        for nt in range(MT):
                            n = h * MT + nt
                            dve.wait_ge(S["mx_scores"], t * (HG * MT) + (n + 2))
                            nc.vector.tensor_reduce(row_max[:, nt, h:h + 1], score_ps[n % 2], AX.X, ALU.max, negate=True)\
                                .then_inc(S["mx_read"], 1)
                    dve.wait_ge(S["mx_read"], t * (HG * MT) + (HG * MT + 2))
                    nc.vector.tensor_copy(shift_hi[:], row_max[:]).then_inc(S["mx_made"], 1)
                    dve.wait_ge(S["mx_made"], t * 3 + 1)
                    nc.vector.tensor_copy(shift_nt[:, 0:MT, 0, :], shift_hi[:].bitcast(F32)).then_inc(S["mx_made"], 1)
                    nc.vector.tensor_tensor(shift_nt[:, 0:MT, 1, :], row_max[:], shift_hi[:].bitcast(F32), ALU.subtract).then_inc(S["mx_made"], 1)
                    dve.wait_ge(S["mx_turned"], t + 1)
                    dve.wait_ge(S["mx_stored"], t * (16 * MT) + 16 * MT)
                    nc.vector.tensor_copy(shift_rows[:], score_ps[2][:, 0:P]).then_inc(S["mx_copied"], 1)

            dve.wait_ge(S["v_copied"], B + 1)

            def load_v(t, part, first=False):
                if not first:
                    dve.wait_ge(S["pv_done"], t * BLOCKS + (3 * BLOCKS // 4 if part == 0 else BLOCKS))
                nc.vector.tensor_copy(v_st[:, 4 * part:4 * part + 4, :, 0:D],
                                      v_all[:, bass.ds(t, 1), 4 * part:4 * part + 4, :].rearrange("p a m (h d) -> p (a m) h d", d=D)
                                      ).then_inc(S["v_loaded"], 1)

            load_v(0, 0, True)
            load_v(0, 1, True)

            def copy_o(t, half):
                dve.wait_ge(S["pv_done"], t * BLOCKS + (BLOCKS + (half + 1) * MT))
                nc.vector.tensor_copy(o_sb[:, half, :], o_ps[half]).then_inc(S["o_copied"], 1)

            def normalise(t, half):
                dve.wait_ge(S["o_turned"], t * 2 + (half + 1))
                o = o_ps[half].rearrange("p (k h d) -> p (k h) d", h=HG, d=32)
                nc.vector.reciprocal(o_rec[:], o[:, :, D:D + 1].rearrange("p a b -> p (a b)")).then_inc(S["norm_chain"], 1)
                dve.wait_ge(S["norm_chain"], t * 2 + (half + 1))
                nc.vector.tensor_tensor(attn_all[:, bass.ds(t, 1), 4 * half:4 * half + 4, :].rearrange("p a k (h d) -> p (a k h) d", d=D),
                                        o[:, :, 0:D], o_rec[:].rearrange("p (a b) -> p a b", b=1).to_broadcast([P, 4 * HG, D]),
                                        ALU.mult).then_inc(S["o_free"], 1)
                dve.wait_ge(S["o_free"], t * 2 + (half + 3))

            def combine(i):
                dve.wait_ge(S["gathered"], i * 128 + 128)
                for c in range(2):
                    for k in range(4):
                        xt = x_all[:, bass.ds(i * 4 + k, 1), :].rearrange("p a c -> p (a c)")
                        ins = nc.vector.scalar_tensor_tensor(xt, gath[:, 4 * c + k, :],
                                                             gates[:, bass.ds(i * 4 + k, 1), c], xt, ALU.mult, ALU.add)
                    done = "combined" if c else "comb_chain"
                    ins.then_inc(S[done], 1)
                    dve.wait_ge(S[done], i * 1 + 1)

            def attention_outputs(t, last, experts):
                copy_o(t, 0)
                normalise(t, 0)
                if experts:
                    combine(t - SPLIT)
                if not last:
                    load_v(t + 1, 0)
                copy_o(t, 1)
                if not last:
                    load_v(t + 1, 1)
                normalise(t, 1)

            with dve.Fori(0, SPLIT) as t:
                attention_outputs(t, False, False)

            def copy_xsT(j, par):
                dve.wait_ge(S["xs_turned"], j + 1)
                nc.vector.tensor_copy(xsT[:, par, :], xs_ps[par][:, 0:ST]).then_inc(S["xsT_made"], 1)

            def finish_y(j, par, first=False):
                e = dve.value_load(expert_i[0:1, bass.ds(j, 1)], min_val=0, max_val=E_ - 1)
                dve.wait_ge(S["l3_done"], j + 1)
                if not first:
                    dve.wait_ge(y_stored[par], (j - par) * 8)
                nc.vector.tensor_tensor(y_sb[:, par], y_ps[par][:, 0:2 * C].rearrange("p (k c) -> p k c", c=C),
                                        b3_sb[:, bass.ds(e, 1), :].to_broadcast([P, 2, C]), ALU.add).then_inc(S["y_made"], 1)

            dve.wait_ge(S["bias_loaded"], 16)
            copy_xsT(0, 0)
            copy_xsT(1, 1)
            finish_y(0, 0, first=True)
            copy_xsT(2, 0)
            finish_y(1, 1, first=True)
            copy_xsT(3, 1)
            with dve.Fori(1, (SLOT_TILES - 1) // 2) as i:
                finish_y(i * 2, 0)
                copy_xsT(i * 2 + 2, 0)
                finish_y(i * 2 + 1, 1)
                copy_xsT(i * 2 + 3, 1)
            finish_y(SLOT_TILES - 1, 0)

            with dve.Fori(SPLIT, STEPS - 1) as t:
                attention_outputs(t, False, True)
            attention_outputs(STEPS - 1, True, True)
            dve.wait_ge(S["o_free"], 2 * STEPS + 2)
            for b in range(B):
                xb = x_all[:, b * BT:(b + 1) * BT, :].rearrange("p k (g c) -> p g k c", g=G)
                nc.vector.tensor_tensor(xb, xb, attn_all[:, b * G:(b + 1) * G, :, :], ALU.add).then_inc(S["out_ready"], 1)

        @block.tensor
        def _(pe):
            pe.sem_inc(S["pv_done"], BLOCKS)
            pe.sem_inc(S["trans_done"], 2)
            pe.sem_inc(S["mx_scores"], 1)
            pe.sem_inc(S["norms_done"], 2)
            pe.wait_ge(S["small_loaded"], 96)
            for k in range(3):
                ins = nc.tensor.transpose(v_ps[:, k * C:(k + 1) * C], w_raw[:, k * C:(k + 1) * C], ident)
            ins = nc.tensor.transpose(v_ps[:, 3 * C:3 * C + 4 * E_], b_raw[:], ident[0:4 * E_, 0:4 * E_])
            ins.then_inc(S["wT_made"], 1)
            pe.wait_ge(S["wT_copied"], 1)
            pe.wait_ge(S["weights_loaded"], 64)

            def norms(b, n):
                pe.wait_ge(S["squares_made"], b * 4 + (n + 3))
                pe.wait_ge(S["norms_read"], b * 4 + (n + 1))
                nc.tensor.matmul(trans_ps[0:H, HALF:N], head_r[:], squares[:, n % 2, :], start=True, stop=True)\
                    .then_inc(S["norms_done"], 1)

            with pe.Fori(0, B) as b:
                pe.wait_ge(S["norms_read"], b * 4 + 1)
                pe.wait_ge(S["xnb_made"], b * 1 + 1)
                pe.wait_ge(S["gate_copied"], b + 1)
                for k in range(BT):
                    ins = nc.tensor.transpose(trans_ps[:, k * C:(k + 1) * C], xnb[:, k, :], ident)
                    if k % 4 == 3:
                        ins.then_inc(S["trans_done"], 1)
                pe.wait_ge(S["xnT_made_v"], b * 1 + 1)
                pe.wait_ge(S["xnT_made_a"], b * 1 + 1)
                pe.wait_ge(S["v_copied"], b + 1)
                for k in range(BT):
                    ins = nc.tensor.matmul(v_ps[:, k * C:(k + 1) * C], xnT[:, k * C:(k + 1) * C], wT[:, 4, :], start=True, stop=True)
                ins.then_inc(S["v_done"], 1)
                for n in range(4):
                    u, m = n % 2, n // 2
                    pe.wait_ge(S["proj_read"], b * 4 + (n + 1))
                    for s in range(2):
                        ins = nc.tensor.matmul(proj_ps[u][:, s * HALF:(s + 1) * HALF], wT[:, 2 * u + s, :],
                                               xnT[:, m * HALF:(m + 1) * HALF], start=True, stop=True)
                    ins.then_inc(S["proj_done"], 1)
                    if n >= 1:
                        norms(b, n - 1)
                for k in range(BT):
                    ins = nc.tensor.matmul(trans_ps[:, k * E_:(k + 1) * E_], xnT[:, k * C:(k + 1) * C], gw_sb[:], start=True, stop=True)
                ins.then_inc(S["gate_done"], 1)
                norms(b, 3)
            pe.wait_ge(S["bound_made"], 1)
            nc.tensor.matmul(trans_ps[0:1, 512:512 + H], bound[:, 2:3], ident[0:H, 0:H], start=True, stop=True).then_inc(S["bound_summed"], 1)
            pe.wait_ge(S["masks_made"], 1)
            pe.wait_ge(S["v_copied"], B + 1)
            masks = rt[:, 8].rearrange("p k e -> p (k e)")
            nc.tensor.matmul(v_ps[:, 0:TILES * E_], before, masks, start=True, stop=True)
            nc.tensor.matmul(v_ps[:, 512:512 + TILES * E_], ones, masks, start=True, stop=True).then_inc(S["prefix_made"], 1)
            pe.wait_ge(S["routed"], 2)

            def scores(t, j, first=False):
                half, mt = divmod(j, MT)
                if j == 0:
                    pe.wait_ge(S["ka_loaded"], t * (16 * QK_LOADS) + 16 * QK_LOADS)
                    pe.wait_ge(S["q0_loaded"], t * (16 * Q_LOADS) + 16 * Q_LOADS)
                if j == 4:
                    pe.wait_ge(S["kb_loaded"], t * (16 * QK_LOADS) + 16 * QK_LOADS)
                if j == MT:
                    pe.wait_ge(S["q1_loaded"], t * (16 * Q_LOADS) + 16 * Q_LOADS)
                for pair in range(2):
                    u = 2 * j + pair
                    if u >= SCORE_RING:
                        pe.wait_ge(S["exp_done"], t * UNITS + (u - SCORE_RING + 1))
                    elif not first and u < 2:
                        pe.wait_ge(S["exp_done"], t * UNITS - (1 - u))
                    for s in range(2):
                        ins = nc.tensor.matmul(score_ps[u % SCORE_RING][:, s * HALF:(s + 1) * HALF],
                                               k_st[:, mt * P:(mt + 1) * P],
                                               q_mv[:, 2 * pair + s, half * HALF:(half + 1) * HALF], start=True, stop=True)
                    ins.then_inc(S["scores_done"], 1)

            def values(t, j):
                half, mt = divmod(j, MT)
                pe.wait_ge(S["exp_done"], t * UNITS + (2 * j + 2))
                if j in (0, 4):
                    pe.wait_ge(S["v_loaded"], t * 2 + (j // 4 + 1))
                if mt == 0:
                    pe.wait_ge(S["o_free"], t * 2 + (half + 1))
                for h in range(HG):
                    ins = nc.tensor.matmul(o_ps[half][32 * h:32 * h + 32, :], v_st[:, mt, h, :],
                                           probs[:, j % PROB_RING, h, :], start=(mt == 0), stop=(mt == MT - 1))
                ins.then_inc(S["pv_done"], 1)

            def turn(t, half):
                pe.wait_ge(S["o_copied"], t * 2 + (half + 1))
                for k in range(4):
                    ins = nc.tensor.transpose(o_ps[half][:, k * P:(k + 1) * P], o_sb[:, half, k * P:(k + 1) * P], ident)
                ins.then_inc(S["o_turned"], 1)

            def step(t, last):
                for j in range(BLOCKS):
                    if j < BLOCKS - 1:
                        scores(t, j + 1)
                    elif not last:
                        scores(t + 1, 0)
                    values(t, j)
                    if j == MT + 2:
                        turn(t, 0)
                turn(t, 1)

            with pe.If(pe.value_load(flag_i[0:1, 0:1], min_val=0, max_val=1)):
                with pe.Fori(0, STEPS) as t:
                    pe.wait_ge(S["mx_loaded"], t * (16 * 30) + 16 * 30)
                    for h in range(HG):
                        for nt in range(MT):
                            n = h * MT + nt
                            pe.wait_ge(S["mx_read"], t * (HG * MT) + (n + 1))
                            for s in range(2):
                                ins = nc.tensor.matmul(score_ps[n % 2][:, s * HALF:(s + 1) * HALF], q_mv[:, h, nt * P:(nt + 1) * P],
                                                       k_st[:, s * HALF:(s + 1) * HALF], start=True, stop=True)
                            ins.then_inc(S["mx_scores"], 1)
                    pe.wait_ge(S["mx_made"], t * 3 + 3)
                    nc.tensor.transpose(score_ps[2][:, 0:P], shift_nt[:].rearrange("p m a h -> p (m a h)"), ident)\
                        .then_inc(S["mx_turned"], 1)
                pe.wait_ge(S["mx_read"], STEPS * HG * MT + 2)
                pe.wait_ge(S["mx_copied"], STEPS)

            scores(0, 0, first=True)
            with pe.Fori(0, SPLIT - 1) as t:
                step(t, False)
            step(SPLIT - 1, True)

            def in_count(j, par):
                return (j - par) * 8 + 16

            def turn_rows(j, par):
                pe.wait_ge(xs_in[par], in_count(j, par))
                for k in range(2):
                    ins = nc.tensor.transpose(xs_ps[par][:, k * P:(k + 1) * P], xs_sb[:, par, k, :], ident)
                ins.then_inc(S["xs_turned"], 1)

            def layer1(j, par):
                pe.wait_ge(w1_in[par], in_count(j, par))
                pe.wait_ge(S["xsT_made"], j + 1)
                for m in range(2):
                    ins = nc.tensor.matmul(h1_ps[par][:, m * ST:(m + 1) * ST], w1_sb[:, par, m * P:(m + 1) * P],
                                           xsT[:, par, :], start=True, stop=True)
                ins.then_inc(S["l1_done"], 1)

            def layer2(j, par):
                pe.wait_ge(w2_in[par], in_count(j, par))
                pe.wait_ge(S["g1_done"], j + 1)
                for m in range(2):
                    for k in range(2):
                        ins = nc.tensor.matmul(h2_ps[par][:, m * ST:(m + 1) * ST], w2_sb[:, par, k, m * P:(m + 1) * P],
                                               h1[:, par, k, :], start=(k == 0), stop=(k == 1))
                ins.then_inc(S["l2_done"], 1)

            def layer3(j, par):
                pe.wait_ge(w3_in[par], in_count(j, par))
                pe.wait_ge(S["g2_done"], j + 1)
                pe.wait_ge(S["y_made"], j + 1)
                for m in range(2):
                    for k in range(2):
                        ins = nc.tensor.matmul(y_ps[par][:, m * C:(m + 1) * C], h2[:, par, k, m * P:(m + 1) * P],
                                               w3_sb[:, par, k, :], start=(k == 0), stop=(k == 1))
                ins.then_inc(S["l3_done"], 1)

            pe.wait_ge(S["o_free"], 2 * SPLIT + 2)
            pe.wait_ge(S["exp_done"], SPLIT * UNITS)
            turn_rows(0, 0)
            layer1(0, 0)
            layer2(0, 0)
            turn_rows(1, 1)
            with pe.Fori(0, (SLOT_TILES - 1) // 2) as i:
                for k in range(2):
                    layer1(i * 2 + (1 + k), 1 - k)
                    layer3(i * 2 + k, k)
                    layer2(i * 2 + (1 + k), 1 - k)
                    turn_rows(i * 2 + (2 + k), k)
            layer3(SLOT_TILES - 1, 0)
            pe.wait_ge(S["xsT_made"], SLOT_ROOM)
            pe.wait_ge(S["y_made"], SLOT_TILES + 2)

            scores(SPLIT, 0, first=True)
            with pe.Fori(SPLIT, STEPS - 1) as t:
                step(t, False)
            step(STEPS - 1, True)


_INS = ['L0_attn_x', 'L0_attn_Wq', 'L0_attn_Wk', 'L0_attn_Wv', 'L0_ffn_w1', 'L0_ffn_b1', 'L0_ffn_w2', 'L0_ffn_b2',
        'L0_ffn_w3', 'L0_ffn_b3', 'L0_ffn_gate_w', 'L0_ffn_gate_b']


def _constants():
    import numpy as np
    d = np.arange(C) % D
    inv = np.power(np.float32(10000.0), (np.float32(-2.0) * np.arange(D // 2, dtype=np.float32) / np.float32(D)).astype(np.float32))
    ang = (np.arange(N, dtype=np.float32)[:, None] * inv.astype(np.float32)[None, :]).astype(np.float32)
    cos, sin = np.cos(ang).astype(np.float32), np.sin(ang).astype(np.float32)
    rope_cos = np.ascontiguousarray(cos[:, d // 2].T)
    rope_sin = np.ascontiguousarray(sin[:, d // 2].T * np.where(d % 2, 1, -1).astype(np.float32)[:, None])
    consts = np.zeros((P, 3 * P + 8 + 40 + 32 + H), np.float32)
    consts[:, 0:P] = np.eye(P)
    consts[:, P:2 * P] = np.arange(P)[:, None] < np.arange(P)[None, :]
    consts[:, 2 * P:3 * P] = 1
    consts[:, 384:392] = E_ - np.arange(E_)
    consts[:, 392:432] = np.arange(40)
    consts[:, 432:464] = ST * np.arange(32)
    consts[:, 464:480] = np.arange(P)[:, None] // D == np.arange(H)[None, :]
    return rope_cos, rope_sin, consts


def kernel(**inputs):
    import numpy as _np
    import concourse.bacc as _bacc
    from concourse import mybir as _mybir
    from concourse.bass_utils import run_bass_kernel_spmd as _run

    nc = _bacc.Bacc("TRN2", target_bir_lowering=False, num_devices=1)
    arrays, args = {}, []
    for name in _INS:
        a = _np.ascontiguousarray(inputs[name])
        arrays[f"in_{name}_dram"] = a
        args.append(nc.dram_tensor(f"in_{name}_dram", a.shape, _mybir.dt.from_np(a.dtype), kind="ExternalInput").ap())
    for name, a in zip(("rope_cos", "rope_sin", "consts"), _constants()):
        arrays[f"in_{name}_dram"] = a
        args.append(nc.dram_tensor(f"in_{name}_dram", a.shape, _mybir.dt.from_np(a.dtype), kind="ExternalInput").ap())
    args.append(nc.dram_tensor("out_0_dram", (B, N, C), F32, kind="ExternalOutput").ap())
    build(nc, *args)
    r = _run(nc, [arrays], core_ids=[0])
    return r.results[0]["out_0_dram"]
```

```python
import concourse.bass as bass
from concourse import mybir
from contextlib import ExitStack

F32 = mybir.dt.float32
F32R = mybir.dt.float32r
I32 = mybir.dt.int32
U32 = mybir.dt.uint32
ACT = mybir.ActivationFunctionType
ALU = mybir.AluOpType
AX = mybir.AxisListType

P = 128
B, N, C = 4, 1024, 128
H, D = 16, 8
HG = 4
G = H // HG
STEPS = B * G
TILES = B * N // P
BT = N // P
HALF = N // 2
MT = N // P
SCALE = float(D) ** -0.5
EPS = 1e-5
E_, HID = 8, 256
ST = 256
SLOT_TILES = (2 * B * N + E_ * (ST - 1)) // ST
SLOT_ROOM = SLOT_TILES + 1
UNITS = 2 * MT * 2
BLOCKS = 2 * MT
SCORE_RING = 3
PROB_RING = 4
SPLIT = 8
SAFE_SCORE = 60.0


def build(nc, x, Wq, Wk, Wv, w1, b1, w2, b2, w3, b3, gw, gb, rope_cos, rope_sin, consts, out):
    ctx = ExitStack()
    with ctx:
        def sb(name, shape, dt=F32):
            return ctx.enter_context(nc.sbuf_tensor(name, shape, dt))

        def sem(name):
            return ctx.enter_context(nc.semaphore(name))

        def dram(name, shape, dt=F32):
            return nc.dram_tensor(name, shape, dt, kind="Internal").ap()

        qhi_d, qlo_d, khi_d, klo_d = (dram(n, (B * C, N)) for n in ("qhi_d", "qlo_d", "khi_d", "klo_d"))
        shift_d = dram("shift_d", (STEPS, 2, HG, N))
        slots_x_d = dram("slots_x_d", (SLOT_ROOM * ST, C))
        slots_y_d = dram("slots_y_d", (SLOT_TILES * ST, C))

        x_all = sb("x_all", [P, TILES, C])
        xn_all = sb("xn_all", [P, TILES, C])
        v_all = sb("v_all", [P, STEPS, MT, HG * D])
        attn_all = sb("attn_all", [P, STEPS, BT, HG * D])
        cst = sb("cst", [P, 3 * P + 8 + 40 + 32 + 32])
        ident, before, ones = cst[:, 0:P], cst[:, P:2 * P], cst[:, 2 * P:3 * P]
        prefer = cst[:, 384:392]
        iota_tile = cst[:, 392:432]
        iota_fill = cst[:, 432:464]
        head_of = cst[:, 464:496]

        k_st = sb("k_st", [P, N], F32R)
        q_mv = sb("q_mv", [P, HG, N], F32R)
        v_st = sb("v_st", [P, MT, HG, 32])
        probs = sb("probs", [P, PROB_RING, HG, HALF])
        o_sb = sb("o_sb", [P, 2, HALF])
        o_rec = sb("o_rec", [P, 4 * HG])

        logits = sb("logits", [P, TILES, E_])
        gates = sb("gates", [P, TILES, 2])
        slot_i = sb("slot_i", [P, 2, TILES], I32)
        expert_i = sb("expert_i", [P, 40], I32)
        gbias = sb("gbias", [P, E_])
        gw_sb = sb("gw_sb", [P, E_])
        b_raw = sb("b_raw", [4 * E_, P])
        b12 = sb("b12", [P, 2, E_, 2])
        b1_sb, b2_sb = b12[:, 0], b12[:, 1]
        b3_sb = sb("b3_sb", [P, E_, C])
        gath = sb("gath", [P, 8, C])

        pr = probs[:].rearrange("p r h n -> p (r h n)")
        cos_sb, sin_sb = pr[:, 0:1024], pr[:, 1024:2048]
        xnb = pr[:, 2048:3072].rearrange("p (k c) -> p k c", c=C)
        xnT = pr[:, 3072:4096]
        t_cos, t_sin = pr[:, 4096:4608], pr[:, 4608:5120]
        rot = pr[:, 5120:6144].rearrange("p (u n) -> p u n", u=2)
        w_raw = pr[:, 6144:6528]
        zeros = sb("zeros", [P, 1024])
        wT = sb("wT", [P, 5, C])
        part_hi = sb("part_hi", [P, 2, HALF], F32R)
        part_lo = sb("part_lo", [P, 2, HALF], F32R)
        stats = sb("stats", [P, TILES, 6])
        mean = sb("mean", [P, TILES])
        std = sb("std", [P, 4, TILES])
        peak = sb("peak", [P, B])
        squares = sb("squares", [P, 2, HALF])
        bound = sb("bound", [P, 1])
        bound_row = sb("bound_row", [1, 4, 32])
        flag_i = sb("flag_i", [1, 1], I32)
        row_max = sb("row_max", [P, MT, HG])
        shift_hi = sb("shift_hi", [P, MT, HG], F32R)
        shift_nt = sb("shift_nt", [P, 2 * MT, 2, HG])
        shift_rows = sb("shift_rows", [P, P])
        rt = sb("rt", [P, 12, TILES, E_])
        rs = sb("rs", [P, 8, TILES])
        rcmp = sb("rcmp", [P, 40, E_])
        r8 = sb("r8", [P, 4, E_])

        w1_sb = sb("w1_sb", [P, 2, HID])
        w2_sb = sb("w2_sb", [P, 2, 2, HID])
        w3_sb = sb("w3_sb", [P, 2, 2, C])
        xs_sb = sb("xs_sb", [P, 2, 2, C])
        xsT = sb("xsT", [P, 2, ST])
        h1 = sb("h1", [P, 2, 2, ST])
        h2 = sb("h2", [P, 2, 2, ST])
        y_sb = sb("y_sb", [P, 2, 2, C])

        ps = ctx.enter_context(nc.psum_tensor("ps", [P, 4096], F32))

        def bank(k, n=1):
            return ps[:, 512 * k:512 * (k + n)]

        trans_ps, v_ps = bank(0, 2), bank(6, 2)
        proj_ps = [bank(2, 2), bank(4, 2)]
        score_ps = [bank(2 * k, 2) for k in range(SCORE_RING)]
        o_ps = [bank(6), bank(7)]
        xs_ps, y_ps = [bank(0), bank(1)], [bank(6), bank(7)]
        h1_ps, h2_ps = [bank(2), bank(3)], [bank(4), bank(5)]

        names = """x_loaded0 x_loaded1 x_loaded2 x_loaded3 small_loaded weights_loaded gate_loaded bias_loaded
            wT_made wT_copied stats_made std_made std_fixed xnb_made xnb_saved xnT_made_v xnT_made_a
            trans_done proj_done proj_read rot_made hi_made lo_made parts_stored0 parts_stored1
            v_done v_copied gate_done gate_copied dve_chain dve_pro_chain
            max_made exp_made masks_made prefix_made counts_read routed zero_made x_zeroed x_scattered
            st_init ka_loaded kb_loaded q0_loaded q1_loaded v_loaded scores_done exp_done pv_done
            o_copied o_turned o_free norm_chain
            w1_in0 w1_in1 w2_in0 w2_in1 w3_in0 w3_in1 xs_in0 xs_in1 xs_turned xsT_made
            l1_done l2_done l3_done g1_done g2_done y_made y_stored0 y_stored1
            squares_made norms_done norms_read bound_made bound_turned flag_made shift_zeroed mx_loaded mx_scores mx_read mx_made mx_turned mx_copied mx_stored
            gathered combined comb_chain out_ready out_stored attn_ended experts_ended""".split()
        S = {n: sem(n) for n in names}
        parts_stored = [S["parts_stored0"], S["parts_stored1"]]
        w1_in, w2_in, w3_in, xs_in, y_stored = ([S[f"{n}{k}"] for k in range(2)]
                                                for n in ("w1_in", "w2_in", "w3_in", "xs_in", "y_stored"))
        QK_LOADS = 3
        Q_LOADS = 3 * HG + 1

        block = ctx.enter_context(nc.Block())

        @block.sync
        def _(sp):
            sp.sem_inc(S["parts_stored0"], 32)
            sp.sem_inc(S["parts_stored1"], 32)
            sp.sem_inc(S["xnb_saved"], 16)
            xv = x.rearrange("b (k p) c -> p b k c", p=P)
            sp.dma_start(x_all[:, 0:BT, :], xv[:, 0]).then_inc(S["x_loaded0"], 16)
            for k, w in enumerate((Wq, Wk, Wv)):
                sp.dma_start(w_raw[:, k * C:(k + 1) * C], w).then_inc(S["small_loaded"], 16)
            sp.dma_start(cst[:], consts).then_inc(S["small_loaded"], 16)
            for k, bias in enumerate((b1, b2)):
                sp.dma_start(b_raw[2 * E_ * k:2 * E_ * (k + 1), :], bias.rearrange("e (h p) -> (e h) p", p=P))\
                    .then_inc(S["small_loaded"], 16)
            sp.dma_start(gw_sb[:], gw).then_inc(S["gate_loaded"], 16)
            sp.dma_start(gbias[:], gb.rearrange("(a e) -> a e", a=1).partition_broadcast(P)).then_inc(S["gate_loaded"], 16)
            for b in range(1, B):
                sp.dma_start(x_all[:, b * BT:(b + 1) * BT, :], xv[:, b]).then_inc(S[f"x_loaded{b}"], 16)
            sp.dma_start(cos_sb, rope_cos).then_inc(S["weights_loaded"], 16)
            sp.dma_start(sin_sb, rope_sin).then_inc(S["weights_loaded"], 16)

            def store_batch(b, between):
                sp.wait_ge(S["xnb_made"], b * 1 + 1)
                sp.dma_start(xn_all[:, bass.ds(b * BT, BT), :], xnb).then_inc(S["xnb_saved"], 16)
                for half in range(2):
                    for u, (hi_d, lo_d) in enumerate(((qhi_d, qlo_d), (khi_d, klo_d))):
                        for dst, src, signal in between[2 * half + u]:
                            sp.dma_start(dst, src).then_inc(signal, 16)
                        sp.wait_ge(S["lo_made"], b * 4 + (2 * half + u + 3))
                        for d, s in ((hi_d, part_hi), (lo_d, part_lo)):
                            sp.dma_start(d[bass.ds(b * C, C), half * HALF:(half + 1) * HALF],
                                         s[:, u, :].bitcast(F32)).then_inc(parts_stored[u], 16)

            with sp.Fori(0, B - 1) as b:
                store_batch(b, [[]] * 4)
            sp.wait_ge(S["st_init"], 5)
            for u in range(2):
                sp.wait_ge(parts_stored[u], 32 + 16 * 4)
            step0 = [(k_st[32 * strip:32 * strip + 32, :].bitcast(F32), src[0:32, :], S["ka_loaded"])
                     for strip, src in enumerate((khi_d, klo_d, khi_d))]
            step0 += [(q_mv[32 * strip + D * h:32 * strip + D * h + D, h, :].bitcast(F32), src[D * h:D * h + D, :], S["q0_loaded"])
                      for strip, src in enumerate((qhi_d, qhi_d, qlo_d)) for h in range(HG)]
            store_batch(B - 1, [step0[0:6], step0[6:9], step0[9:12], step0[12:15]])
            sp.sem_inc(S["kb_loaded"], 16 * QK_LOADS)
            sp.sem_inc(S["q0_loaded"], 16)
            sp.sem_inc(S["q1_loaded"], 16 * Q_LOADS)

            def load_k(t, part, signal):
                cols = slice(part * HALF, (part + 1) * HALF)
                for strip, src in enumerate((khi_d, klo_d, khi_d)):
                    sp.dma_start(k_st[32 * strip:32 * strip + 32, cols].bitcast(F32),
                                 src[bass.ds(t * 32, 32), cols]).then_inc(signal, 16)

            def load_q(t, half, signal):
                cols = slice(half * HALF, (half + 1) * HALF)
                for strip, src in enumerate((qhi_d, qhi_d, qlo_d)):
                    for h in range(HG):
                        r = 32 * strip + D * h
                        sp.dma_start(q_mv[r:r + D, h, cols].bitcast(F32),
                                     src[bass.ds(t * 32 + D * h, D), cols]).then_inc(signal, 16)

            def load_shift(t, half, signal):
                cols = slice(half * HALF, (half + 1) * HALF)
                sp.dma_start(q_mv[3 * 32:3 * 32 + 2, :, cols].bitcast(F32),
                             shift_d[bass.ds(t, 1), :, :, cols].rearrange("t a h n -> (t a) h n")).then_inc(signal, 16)

            sp.wait_ge(S["zero_made"], 1)
            sp.dma_start(shift_d.rearrange("t a h (c n) -> (t a h) c n", n=N),
                         zeros[:].rearrange("p (c n) -> p c n", n=N)).then_inc(S["shift_zeroed"], 16)
            sp.wait_ge(S["flag_made"], 1)
            with sp.If(sp.value_load(flag_i[0:1, 0:1], min_val=0, max_val=1)):
                sp.wait_ge(S["ka_loaded"], 16 * QK_LOADS)
                sp.wait_ge(S["q0_loaded"], 16 * Q_LOADS)
                for u in range(2):
                    sp.wait_ge(parts_stored[u], 32 + 16 * 4 * B)
                with sp.Fori(0, STEPS) as t:
                    sp.wait_ge(S["mx_scores"], t * (HG * MT) + 1)
                    for part in range(2):
                        load_k(t, part, S["mx_loaded"])
                        load_q(t, part, S["mx_loaded"])
                sp.wait_ge(S["mx_stored"], 16 * MT * (STEPS + 1))
                for part in range(2):
                    load_k(0, part, S["mx_loaded"])
                    load_q(0, part, S["mx_loaded"])
                    load_shift(0, part, S["mx_loaded"])

            sp.dma_start(b3_sb[:].rearrange("p e c -> p (e c)"),
                         b3.rearrange("(a e) c -> a (e c)", a=1).partition_broadcast(P)).then_inc(S["bias_loaded"], 16)
            for r in range(SLOT_ROOM // 4):
                sp.dma_start(slots_x_d[r * 4 * ST:(r + 1) * 4 * ST, :].rearrange("(p j) c -> p (j c)", p=P),
                             zeros[:]).then_inc(S["x_zeroed"], 16)
            sp.wait_ge(S["shift_zeroed"], 16)
            for u in range(2):
                sp.wait_ge(parts_stored[u], 32 + 16 * 4 * B)

            def attention_loads(lo, hi):
                with sp.Fori(lo, hi) as t:
                    sp.wait_ge(S["scores_done"], t * UNITS + UNITS // 2)
                    load_q(t + 1, 0, S["q0_loaded"])
                    load_shift(t + 1, 0, S["q0_loaded"])
                    sp.wait_ge(S["scores_done"], t * UNITS + 3 * UNITS // 4)
                    load_k(t + 1, 0, S["ka_loaded"])
                    sp.wait_ge(S["scores_done"], t * UNITS + UNITS)
                    load_k(t + 1, 1, S["kb_loaded"])
                    load_q(t + 1, 1, S["q1_loaded"])
                    load_shift(t + 1, 1, S["q1_loaded"])

            attention_loads(0, SPLIT - 2)

            sp.wait_ge(S["x_scattered"], 16 * 2 * TILES)
            sp.wait_ge(S["routed"], 2)

            def expert_of(j):
                return sp.value_load(expert_i[0:1, bass.ds(j, 1)], min_val=0, max_val=E_ - 1)

            def load_rows(j, par, first=False):
                if not first:
                    sp.wait_ge(S["xs_turned"], j - 1)
                sp.dma_start(xs_sb[:, par], slots_x_d[bass.ds(j * ST, ST), :].rearrange("(k p) c -> p k c", p=P)).then_inc(xs_in[par], 16)

            def load_w1(j, par, e, first=False):
                if not first:
                    sp.wait_ge(S["l1_done"], j * 2 - 2)
                sp.dma_start(w1_sb[:, par], w1[bass.ds(e, 1)].rearrange("a p n -> p (a n)")).then_inc(w1_in[par], 16)

            def load_w2(j, par, e, first=False):
                if not first:
                    sp.wait_ge(S["l2_done"], j * 2 - 2)
                sp.dma_start(w2_sb[:, par], w2[bass.ds(e, 1)].rearrange("a (k p) n -> p (a k) n", p=P)).then_inc(w2_in[par], 16)

            def load_w3(j, par, first=False):
                e = expert_of(j)
                if not first:
                    sp.wait_ge(S["l3_done"], j - 1)
                sp.dma_start(w3_sb[:, par], w3[bass.ds(e, 1)].rearrange("a (k p) n -> p (a k) n", p=P)).then_inc(w3_in[par], 16)

            for j in range(2):
                e = expert_of(j)
                load_rows(j, j, True)
                load_w1(j, j, e, True)
                load_w2(j, j, e, True)
                load_w3(j, j, True)
            attention_loads(SPLIT - 2, SPLIT)

            load_rows(2, 0)
            load_w1(2, 0, expert_of(2))
            load_w2(2, 0, expert_of(2))
            with sp.Fori(0, (SLOT_TILES - 3) // 2) as i:
                load_rows(i * 2 + 3, 1)
                e = expert_of(i * 2 + 3)
                load_w1(i * 2 + 3, 1, e)
                load_w3(i * 2 + 2, 0)
                load_w2(i * 2 + 3, 1, e)
                load_rows(i * 2 + 4, 0)
                e = expert_of(i * 2 + 4)
                load_w1(i * 2 + 4, 0, e)
                load_w3(i * 2 + 3, 1)
                load_w2(i * 2 + 4, 0, e)
            load_rows(SLOT_TILES, 1)
            load_w3(SLOT_TILES - 1, 0)

            attention_loads(SPLIT, STEPS - 1)

            ov = out.rearrange("b (k p) c -> p b k c", p=P)
            for n, (tile, tiles) in enumerate([(b * BT, BT) for b in range(B - 1)] + [((B - 1) * BT, BT // 2), (TILES - BT // 2, BT // 2)]):
                sp.wait_ge(S["out_ready"], n + 1)
                sp.dma_start(ov[:, tile // BT, tile % BT:tile % BT + tiles, :], x_all[:, tile:tile + tiles, :]).then_inc(S["out_stored"], 16)
            sp.wait_ge(S["out_stored"], 16 * (B + 1))

        @block.gpsimd
        def _(pool):
            pool.sem_inc(S["lo_made"], 2)
            nc.gpsimd.memset(zeros[:], 0.0).then_inc(S["zero_made"], 1)
            nc.gpsimd.memset(v_st[:], 0.0).then_inc(S["st_init"], 1)
            nc.gpsimd.memset(shift_nt[:], 0.0).then_inc(S["st_init"], 1)
            nc.gpsimd.memset(q_mv[:].bitcast(F32), 0.0).then_inc(S["st_init"], 1)
            pool.wait_ge(S["st_init"], 4)
            nc.gpsimd.memset(v_st[:, :, :, D:D + 1], 1.0).then_inc(S["st_init"], 1)
            with pool.Fori(0, B) as b:
                for n in range(4):
                    u, m = n % 2, n // 2
                    pool.wait_ge(S["hi_made"], b * 4 + (n + 1))
                    pool.wait_ge(parts_stored[u], b * 64 + 32 * (m + 1))
                    nc.gpsimd.tensor_tensor(part_lo[:, u, :], rot[:, u, :], part_hi[:, u, :].bitcast(F32),
                                            ALU.subtract).then_inc(S["lo_made"], 1)
            pool.wait_ge(S["x_zeroed"], 16 * (SLOT_ROOM // 4))
            pool.wait_ge(S["xnb_saved"], 16 + 16 * B)
            pool.wait_ge(S["routed"], 2)
            for i in range(TILES):
                for c in range(2):
                    nc.gpsimd.indirect_dma_start(
                        out=slots_x_d, out_offset=bass.IndirectOffsetOnAxis(ap=slot_i[:, c, i:i + 1].bitcast(U32), axis=0),
                        in_=xn_all[:, i, :], in_offset=None).then_inc(S["x_scattered"], 16)
            def store_y(j, par):
                pool.wait_ge(S["y_made"], j + 3)
                pool.dma_start(slots_y_d[bass.ds(j * ST, ST), :].rearrange("(k p) c -> p k c", p=P),
                               y_sb[:, par]).then_inc(y_stored[par], 16)

            with pool.Fori(0, (SLOT_TILES - 1) // 2) as i:
                store_y(i * 2, 0)
                store_y(i * 2 + 1, 1)
            store_y(SLOT_TILES - 1, 0)
            pool.wait_ge(y_stored[0], 16 * ((SLOT_TILES + 1) // 2))
            pool.wait_ge(y_stored[1], 16 * (SLOT_TILES // 2))
            for i in range(TILES // 4):
                if i >= 1:
                    pool.wait_ge(S["combined"], i)
                for c in range(2):
                    for k in range(4):
                        nc.gpsimd.indirect_dma_start(
                            out=gath[:, 4 * c + k, :], out_offset=None, in_=slots_y_d,
                            in_offset=bass.IndirectOffsetOnAxis(ap=slot_i[:, c, 4 * i + k:4 * i + k + 1].bitcast(U32), axis=0))\
                            .then_inc(S["gathered"], 16)

        @block.scalar
        def _(act):
            act.sem_inc(S["v_copied"], 1)
            act.sem_inc(S["squares_made"], 2)
            def roots(lo, hi, n):
                act.wait_ge(S["stats_made"], n)
                nc.scalar.activation(std[:, 0, lo:hi], std[:, 1, lo:hi], ACT.Sqrt).then_inc(S["std_made"], 1)

            roots(0, BT, 1)
            act.wait_ge(S["std_fixed"], 1)
            def normalise_rows(b):
                act.wait_ge(S["trans_done"], b * 2 + 2)
                act.wait_ge(S["xnb_saved"], b * 16 + 16)
                for k in range(BT):
                    ins = nc.scalar.activation(xnb[:, k, :], x_all[:, bass.ds(b * BT + k, 1), :].rearrange("p a c -> p (a c)"),
                                               ACT.Identity, bias=std[:, 3, bass.ds(b * BT + k, 1)],
                                               scale=std[:, 2, bass.ds(b * BT + k, 1)])
                ins.then_inc(S["xnb_made"], 1)

            def batch(b, last):
                act.wait_ge(S["trans_done"], b * 2 + 4)
                nc.scalar.activation(xnT[:, HALF:N], trans_ps[:, HALF:N], ACT.Copy).then_inc(S["xnT_made_a"], 1)
                for n in range(4):
                    u, m = n % 2, n // 2
                    act.wait_ge(S["rot_made"], b * 4 + (n + 1))
                    act.wait_ge(parts_stored[u], b * 64 + 32 * (m + 1))
                    nc.scalar.activation(part_hi[:, u, :], rot[:, u, :], ACT.Copy).then_inc(S["hi_made"], 1)
                    act.wait_ge(S["norms_done"], b * 4 + (n + 1))
                    nc.scalar.activation(squares[:, u, :], rot[:, u, :], ACT.Square).then_inc(S["squares_made"], 1)
                    if n == 0:
                        act.wait_ge(S["v_done"], b + 1)
                        nc.scalar.activation(v_all[:, bass.ds(b * G, G), :, :].rearrange("p g m c -> p m g c"),
                                             v_ps.rearrange("p (m g c) -> p m g c", g=G, c=HG * D), ACT.Copy).then_inc(S["v_copied"], 1)
                    if n == 1 and not last:
                        act.wait_ge(S["std_fixed"], 2)
                        normalise_rows(b + 1)

            normalise_rows(0)
            roots(BT, TILES, 2)
            with act.Fori(0, B - 1) as b:
                batch(b, False)
            batch(B - 1, True)
            act.sem_inc(S["mx_stored"], 16 * MT)
            act.wait_ge(S["flag_made"], 1)
            act.wait_ge(S["max_made"], 1)
            nc.scalar.activation(rt[:, 1], rt[:, 0], ACT.Exp).then_inc(S["exp_made"], 1)

            with act.If(act.value_load(flag_i[0:1, 0:1], min_val=0, max_val=1)):
                act.wait_ge(S["shift_zeroed"], 16)
                with act.Fori(0, STEPS) as t:
                    act.wait_ge(S["mx_copied"], t + 1)
                    for nt in range(MT):
                        act.dma_start(shift_d[bass.ds(t, 1), :, :, nt * P:(nt + 1) * P].rearrange("t a h n -> (t a h) n"),
                                      shift_rows[nt * 2 * HG:(nt + 1) * 2 * HG, :]).then_inc(S["mx_stored"], 16)

            def attention_exps(t):
                for u in range(UNITS):
                    j, pair = divmod(u, 2)
                    act.wait_ge(S["scores_done"], t * UNITS + (u + 1))
                    if pair == 0:
                        act.wait_ge(S["pv_done"], t * BLOCKS + (BLOCKS + j + 1 - PROB_RING))
                    nc.scalar.activation(probs[:, j % PROB_RING, 2 * pair:2 * pair + 2, :],
                                         score_ps[u % SCORE_RING].rearrange("p (h n) -> p h n", h=2),
                                         ACT.Exp, scale=SCALE).then_inc(S["exp_done"], 1)

            with act.Fori(0, SPLIT) as t:
                attention_exps(t)

            def gelus(j, par):
                e = act.value_load(expert_i[0:1, bass.ds(j, 1)], min_val=0, max_val=E_ - 1)
                for ready, signal, src, dst, bias in (("l1_done", "g1_done", h1_ps, h1, b1_sb), ("l2_done", "g2_done", h2_ps, h2, b2_sb)):
                    for k in range(2):
                        act.wait_ge(S[ready], j * 2 + (k + 1))
                        ins = nc.scalar.activation(dst[:, par, k, :], src[k][:, 0:ST], ACT.Gelu, bias=bias[:, bass.ds(e, 1), k])
                    ins.then_inc(S[signal], 1)

            act.wait_ge(S["routed"], 2)
            act.wait_ge(S["wT_copied"], 1)
            gelus(0, 0)
            with act.Fori(0, (SLOT_TILES - 1) // 2) as i:
                gelus(i * 2 + 1, 1)
                gelus(i * 2 + 2, 0)
            with act.Fori(SPLIT, STEPS) as t:
                attention_exps(t)

        @block.vector
        def _(dve):
            links = {}

            def link(ins, chain="dve_chain", base=None):
                links[chain] = links.get(chain, 0) + 1
                ins.then_inc(S[chain], 1)
                dve.wait_ge(S[chain], links[chain] if base is None else base + links[chain])

            dve.sem_inc(S["proj_read"], 2)
            dve.sem_inc(S["mx_read"], 2)
            dve.sem_inc(S["norms_read"], 1)
            dve.sem_inc(S["gate_copied"], 1)
            dve.sem_inc(S["o_free"], 2)
            dve.sem_inc(S["y_made"], 2)
            nc.vector.memset(k_st[96:128, :].bitcast(F32), 1.0).then_inc(S["st_init"], 1)
            def statistics(lo, hi):
                for k in range(lo, hi):
                    if k % BT == 0:
                        dve.wait_ge(S[f"x_loaded{k // BT}"], 16)
                    nc.vector.bn_stats(stats[:, k, :], x_all[:, k, :]).then_inc(S["dve_pro_chain"], 1)
                dve.wait_ge(S["dve_pro_chain"], hi)
                t = slice(lo, hi)
                link(nc.vector.tensor_tensor(std[:, 0, t], stats[:, t, 1], stats[:, t, 4], ALU.add))
                nc.vector.tensor_scalar(mean[:, t], std[:, 0, t], 0.5, None, ALU.mult)
                link(nc.vector.tensor_tensor(std[:, 1, t], stats[:, t, 1], stats[:, t, 4], ALU.subtract))
                link(nc.vector.scalar_tensor_tensor(std[:, 2, t], std[:, 1, t], 0.25, std[:, 1, t], ALU.mult, ALU.mult))
                link(nc.vector.tensor_tensor(std[:, 3, t], stats[:, t, 2], stats[:, t, 5], ALU.add))
                link(nc.vector.scalar_tensor_tensor(std[:, 0, t], std[:, 3, t], 1.0 / C, std[:, 2, t], ALU.mult, ALU.add))
                nc.vector.tensor_scalar(std[:, 1, t], std[:, 0, t], EPS, None, ALU.add).then_inc(S["stats_made"], 1)

            def invert(lo, hi, n):
                t = slice(lo, hi)
                dve.wait_ge(S["std_made"], n)
                link(nc.vector.reciprocal(std[:, 2, t], std[:, 0, t]))
                link(nc.vector.tensor_tensor(std[:, 3, t], std[:, 1, t], std[:, 2, t], ALU.mult))
                link(nc.vector.tensor_tensor(std[:, 2, t], std[:, 3, t], std[:, 0, t], ALU.add))
                link(nc.vector.tensor_scalar(std[:, 3, t], std[:, 2, t], 0.5, None, ALU.mult))
                link(nc.vector.reciprocal(std[:, 2, t], std[:, 3, t]))
                nc.vector.scalar_tensor_tensor(std[:, 3, t], mean[:, t], -1.0, std[:, 2, t], ALU.mult, ALU.mult)\
                    .then_inc(S["std_fixed"], 1)

            statistics(0, BT)
            invert(0, BT, 1)
            dve.wait_ge(S["wT_made"], 1)
            for k in range(3):
                src = v_ps[:, k * C:(k + 1) * C]
                ins = nc.vector.tensor_copy(wT[:, 2 * k, :], src)
                if k < 2:
                    for o in range(2):
                        ins = nc.vector.tensor_copy(wT[:, 2 * k + 1, o::2], src[:, 1 - o::2])
            ins = nc.vector.tensor_copy(b12[:].rearrange("p l e h -> p (l e h)"), v_ps[:, 3 * C:3 * C + 4 * E_])
            ins.then_inc(S["wT_copied"], 1)
            statistics(BT, TILES)
            def copy_xnT(b):
                dve.wait_ge(S["trans_done"], b * 2 + 3)
                nc.vector.tensor_copy(xnT[:, 0:HALF], trans_ps[:, 0:HALF]).then_inc(S["xnT_made_v"], 1)

            def rotate(b, last):
                for n in range(4):
                    u, m = n % 2, n // 2
                    dve.wait_ge(S["proj_done"], b * 4 + (n + 1))
                    cols = slice(m * HALF, (m + 1) * HALF)
                    nc.vector.tensor_tensor(t_cos, proj_ps[u][:, 0:HALF], cos_sb[:, cols], ALU.mult)
                    ins = nc.vector.tensor_tensor(t_sin, proj_ps[u][:, HALF:N], sin_sb[:, cols], ALU.mult)
                    ins.then_inc(S["proj_read"], 1)
                    dve.wait_ge(S["proj_read"], b * 4 + (n + 3))
                    dve.wait_ge(S["lo_made"], b * 4 + (n + 1))
                    dve.wait_ge(S["squares_made"], b * 4 + (n + 1))
                    nc.vector.tensor_tensor(rot[:, u, :], t_cos, t_sin, ALU.add).then_inc(S["rot_made"], 1)
                    dve.wait_ge(S["rot_made"], b * 4 + (n + 1))
                dve.wait_ge(S["gate_done"], b * 1 + 1)
                nc.vector.tensor_tensor(logits[:, bass.ds(b * BT, BT), :],
                                        v_ps[:, 0:BT * E_].rearrange("p (k e) -> p k e", e=E_),
                                        gbias[:].rearrange("p (a e) -> p a e", a=1).to_broadcast([P, BT, E_]), ALU.add).then_inc(S["gate_copied"], 1)
                if not last:
                    copy_xnT(b + 1)
                dve.wait_ge(S["norms_done"], b * 4 + 6)
                nc.vector.tensor_reduce(peak[:, bass.ds(b, 1)], v_ps[:, HALF:N], AX.X, ALU.max).then_inc(S["norms_read"], 1)

            copy_xnT(0)
            invert(BT, TILES, 2)
            dve.wait_ge(S["gate_loaded"], 32)
            dve.wait_ge(S["weights_loaded"], 32)
            with dve.Fori(0, B - 1) as b:
                rotate(b, False)
            rotate(B - 1, True)
            dve.wait_ge(S["gate_copied"], B + 1)

            def per_tile(a):
                return a.rearrange("p (k a) -> p k a", a=1).to_broadcast([P, TILES, E_])

            link(nc.vector.tensor_reduce(rs[:, 0], logits[:], AX.X, ALU.max))
            nc.vector.tensor_tensor(rt[:, 0], logits[:], per_tile(rs[:, 0]), ALU.subtract).then_inc(S["max_made"], 1)
            dve.wait_ge(S["norms_read"], B + 1)
            nc.vector.tensor_reduce(bound[:], peak[:], AX.X, ALU.max).then_inc(S["bound_made"], 1)
            dve.wait_ge(S["bound_turned"], 1)
            tops = trans_ps[0:1, HALF:HALF + P].rearrange("p (n h) -> p n h", h=32)
            link(nc.vector.tensor_copy(bound_row[:, 0:2], tops[:, 0:2]))
            link(nc.vector.tensor_tensor(bound_row[:, 2:4], bound_row[:, 0:2], tops[:, 2:4], ALU.max))
            link(nc.vector.tensor_tensor(bound_row[:, 0], bound_row[:, 2], bound_row[:, 3], ALU.mult))
            link(nc.vector.tensor_reduce(bound_row[:, 1, 0:1], bound_row[:, 0], AX.X, ALU.max))
            link(nc.vector.tensor_scalar(bound_row[:, 2, 0:1], bound_row[:, 1, 0:1], (SAFE_SCORE / SCALE) ** 2, None, ALU.is_le))
            nc.vector.tensor_scalar(flag_i[:], bound_row[:, 2, 0:1], -1.0, 1.0, ALU.mult, ALU.add).then_inc(S["flag_made"], 1)

            dve.wait_ge(S["flag_made"], 1)
            with dve.If(dve.value_load(flag_i[0:1, 0:1], min_val=0, max_val=1)):
                with dve.Fori(0, STEPS) as t:
                    for h in range(HG):
                        for nt in range(MT):
                            n = h * MT + nt
                            dve.wait_ge(S["mx_scores"], t * (HG * MT) + (n + 2))
                            nc.vector.tensor_reduce(row_max[:, nt, h:h + 1], score_ps[n % 2], AX.X, ALU.max, negate=True)\
                                .then_inc(S["mx_read"], 1)
                    dve.wait_ge(S["mx_read"], t * (HG * MT) + (HG * MT + 2))
                    nc.vector.tensor_copy(shift_hi[:], row_max[:]).then_inc(S["mx_made"], 1)
                    dve.wait_ge(S["mx_made"], t * 3 + 1)
                    nc.vector.tensor_copy(shift_nt[:, 0:MT, 0, :], shift_hi[:].bitcast(F32)).then_inc(S["mx_made"], 1)
                    nc.vector.tensor_tensor(shift_nt[:, 0:MT, 1, :], row_max[:], shift_hi[:].bitcast(F32), ALU.subtract).then_inc(S["mx_made"], 1)
                    dve.wait_ge(S["mx_turned"], t + 1)
                    dve.wait_ge(S["mx_stored"], t * (16 * MT) + 16 * MT)
                    nc.vector.tensor_copy(shift_rows[:], score_ps[2][:, 0:P]).then_inc(S["mx_copied"], 1)

            dve.wait_ge(S["v_copied"], B + 1)

            def load_v(t, part, first=False):
                if not first:
                    dve.wait_ge(S["pv_done"], t * BLOCKS + (3 * BLOCKS // 4 if part == 0 else BLOCKS))
                nc.vector.tensor_copy(v_st[:, 4 * part:4 * part + 4, :, 0:D],
                                      v_all[:, bass.ds(t, 1), 4 * part:4 * part + 4, :].rearrange("p a m (h d) -> p (a m) h d", d=D)
                                      ).then_inc(S["v_loaded"], 1)

            load_v(0, 0, True)
            load_v(0, 1, True)

            def copy_o(t, half):
                dve.wait_ge(S["pv_done"], t * BLOCKS + (BLOCKS + (half + 1) * MT))
                nc.vector.tensor_copy(o_sb[:, half, :], o_ps[half]).then_inc(S["o_copied"], 1)

            def normalise(t, half):
                dve.wait_ge(S["o_turned"], t * 2 + (half + 1))
                o = o_ps[half].rearrange("p (k h d) -> p (k h) d", h=HG, d=32)
                nc.vector.reciprocal(o_rec[:], o[:, :, D:D + 1].rearrange("p a b -> p (a b)")).then_inc(S["norm_chain"], 1)
                dve.wait_ge(S["norm_chain"], t * 2 + (half + 1))
                nc.vector.tensor_tensor(attn_all[:, bass.ds(t, 1), 4 * half:4 * half + 4, :].rearrange("p a k (h d) -> p (a k h) d", d=D),
                                        o[:, :, 0:D], o_rec[:].rearrange("p (a b) -> p a b", b=1).to_broadcast([P, 4 * HG, D]),
                                        ALU.mult).then_inc(S["o_free"], 1)
                dve.wait_ge(S["o_free"], t * 2 + (half + 3))

            def combine(i):
                dve.wait_ge(S["gathered"], i * 128 + 128)
                for c in range(2):
                    for k in range(4):
                        xt = x_all[:, bass.ds(i * 4 + k, 1), :].rearrange("p a c -> p (a c)")
                        ins = nc.vector.scalar_tensor_tensor(xt, gath[:, 4 * c + k, :],
                                                             gates[:, bass.ds(i * 4 + k, 1), c], xt, ALU.mult, ALU.add)
                    done = "combined" if c else "comb_chain"
                    ins.then_inc(S[done], 1)
                    dve.wait_ge(S[done], i * 1 + 1)

            def finish_rows(tile, tiles):
                b = tile // BT
                k = tile % BT
                xb = x_all[:, tile:tile + tiles, :].rearrange("p k (g c) -> p g k c", g=G)
                nc.vector.tensor_tensor(xb, xb, attn_all[:, b * G:(b + 1) * G, k:k + tiles, :], ALU.add).then_inc(S["out_ready"], 1)

            def attention_outputs(t, last, experts, before_last_copy=None):
                copy_o(t, 0)
                normalise(t, 0)
                if experts:
                    combine(t - SPLIT)
                if not last:
                    load_v(t + 1, 0)
                if before_last_copy:
                    before_last_copy()
                copy_o(t, 1)
                if not last:
                    load_v(t + 1, 1)
                normalise(t, 1)

            dve.wait_ge(S["exp_made"], 1)
            link(nc.vector.tensor_reduce(rs[:, 1], rt[:, 1], AX.X, ALU.add))
            link(nc.vector.reciprocal(rs[:, 2], rs[:, 1]))
            link(nc.vector.tensor_tensor(rt[:, 2], rt[:, 1], per_tile(rs[:, 2]), ALU.mult))
            prefer_b = prefer.rearrange("p (a e) -> p a e", a=1).to_broadcast([P, TILES, E_])
            for c in range(2):
                src, one = rt[:, 2 + c], rt[:, 4 + c]
                link(nc.vector.tensor_reduce(gates[:, :, c], src, AX.X, ALU.max))
                link(nc.vector.tensor_tensor(rt[:, 6], src, per_tile(gates[:, :, c]), ALU.is_equal))
                link(nc.vector.tensor_tensor(rt[:, 7], rt[:, 6], prefer_b, ALU.mult))
                link(nc.vector.tensor_reduce(rs[:, 3], rt[:, 7], AX.X, ALU.max))
                link(nc.vector.tensor_tensor(one, rt[:, 7], per_tile(rs[:, 3]), ALU.is_equal))
                if c == 0:
                    link(nc.vector.scalar_tensor_tensor(rt[:, 3], one, -2.0, src, ALU.mult, ALU.add))
            nc.vector.tensor_tensor(rt[:, 8], rt[:, 4], rt[:, 5], ALU.add).then_inc(S["masks_made"], 1)
            dve.wait_ge(S["prefix_made"], 1)
            pre = rt[:, 11]
            nc.vector.tensor_copy(pre, o_ps[1][:, 0:TILES * E_].rearrange("p (k e) -> p k e", e=E_)).then_inc(S["counts_read"], 1)
            nc.vector.tensor_copy(rt[:, 9], o_ps[1][:, TILES * E_:2 * TILES * E_].rearrange("p (k e) -> p k e", e=E_))\
                .then_inc(S["counts_read"], 1)
            dve.wait_ge(S["counts_read"], 2)
            nc.vector.memset(rt[:, 7], 1.0)
            link(nc.vector.memset(rcmp[:], 1.0))
            for e in range(E_):
                ins = nc.vector.tensor_tensor_scan(rt[:, 10, :, e], rt[:, 7, :, e], rt[:, 9, :, e], 0.0, ALU.mult, ALU.add)
            link(ins)
            fill_b = iota_fill.rearrange("p (k a) -> p k a", a=1).to_broadcast([P, TILES, E_])
            count_b = rt[:, 10, TILES - 1:TILES, :].to_broadcast([P, TILES, E_])
            link(nc.vector.tensor_tensor(rt[:, 6], count_b, fill_b, ALU.is_gt))
            link(nc.vector.tensor_reduce(r8[:, 0], rt[:, 6].rearrange("p k e -> p e k"), AX.X, ALU.add))
            link(nc.vector.tensor_tensor_scan(r8[:, 1], rcmp[:, 0, :], r8[:, 0], 0.0, ALU.mult, ALU.add))
            link(nc.vector.tensor_tensor(r8[:, 2], r8[:, 1], r8[:, 0], ALU.subtract))
            link(nc.vector.tensor_scalar(r8[:, 3], r8[:, 2], float(ST), None, ALU.mult))
            link(nc.vector.tensor_tensor(rt[:, 6], rt[:, 10], rt[:, 9], ALU.subtract))
            link(nc.vector.tensor_tensor(rt[:, 7], rt[:, 6], pre, ALU.add))
            link(nc.vector.tensor_tensor(rt[:, 6], rt[:, 7], r8[:, 3:4].to_broadcast([P, TILES, E_]), ALU.add))
            for c in range(2):
                link(nc.vector.tensor_tensor(rt[:, 7], rt[:, 4 + c], rt[:, 6], ALU.mult))
                link(nc.vector.tensor_reduce(rs[:, 4 + c], rt[:, 7], AX.X, ALU.add))
            nc.vector.tensor_copy(slot_i[:], rs[:, 4:6]).then_inc(S["routed"], 1)
            link(nc.vector.tensor_tensor(rcmp[:], r8[:, 1:2].to_broadcast([P, 40, E_]),
                                         iota_tile.rearrange("p (k a) -> p k a", a=1).to_broadcast([P, 40, E_]), ALU.is_le))
            link(nc.vector.tensor_reduce(rt[:, 0].rearrange("p k e -> p (k e)")[:, 0:40], rcmp[:], AX.X, ALU.add))
            nc.vector.tensor_scalar(expert_i[:], rt[:, 0].rearrange("p k e -> p (k e)")[:, 0:40], float(E_ - 1), None, ALU.min)\
                .then_inc(S["routed"], 1)
            dve.wait_ge(S["routed"], 2)

            def copy_xsT(j, par):
                dve.wait_ge(S["xs_turned"], j + 1)
                nc.vector.tensor_copy(xsT[:, par, :], xs_ps[par][:, 0:ST]).then_inc(S["xsT_made"], 1)

            def finish_y(j, par, first=False):
                e = dve.value_load(expert_i[0:1, bass.ds(j, 1)], min_val=0, max_val=E_ - 1)
                dve.wait_ge(S["l3_done"], j + 1)
                if not first:
                    dve.wait_ge(y_stored[par], (j - par) * 8)
                nc.vector.tensor_tensor(y_sb[:, par], y_ps[par][:, 0:2 * C].rearrange("p (k c) -> p k c", c=C),
                                        b3_sb[:, bass.ds(e, 1), :].to_broadcast([P, 2, C]), ALU.add).then_inc(S["y_made"], 1)

            def first_rows():
                copy_xsT(0, 0)
                copy_xsT(1, 1)

            with dve.Fori(0, SPLIT - 1) as t:
                attention_outputs(t, False, False)
            attention_outputs(SPLIT - 1, False, False, first_rows)
            dve.wait_ge(S["bias_loaded"], 16)
            copy_xsT(2, 0)
            finish_y(0, 0, first=True)
            copy_xsT(3, 1)
            finish_y(1, 1, first=True)
            with dve.Fori(1, (SLOT_TILES - 1) // 2) as i:
                for par in range(2):
                    copy_xsT(i * 2 + (2 + par), par)
                    finish_y(i * 2 + par, par)
            finish_y(SLOT_TILES - 1, 0)

            with dve.Fori(SPLIT, STEPS - 1) as t:
                attention_outputs(t, False, True)
            last = STEPS - 1
            copy_o(last, 0)
            normalise(last, 0)
            combine(last - SPLIT)
            for b in range(B - 1):
                finish_rows(b * BT, BT)
            finish_rows((B - 1) * BT, BT // 2)
            copy_o(last, 1)
            normalise(last, 1)
            finish_rows((B - 1) * BT + BT // 2, BT // 2)

        @block.tensor
        def _(pe):
            pe.sem_inc(S["pv_done"], BLOCKS)
            pe.sem_inc(S["trans_done"], 2)
            pe.sem_inc(S["mx_scores"], 1)
            pe.sem_inc(S["norms_done"], 2)
            pe.wait_ge(S["small_loaded"], 96)
            for k in range(3):
                ins = nc.tensor.transpose(v_ps[:, k * C:(k + 1) * C], w_raw[:, k * C:(k + 1) * C], ident)
            ins = nc.tensor.transpose(v_ps[:, 3 * C:3 * C + 4 * E_], b_raw[:], ident[0:4 * E_, 0:4 * E_])
            ins.then_inc(S["wT_made"], 1)
            pe.wait_ge(S["wT_copied"], 1)
            pe.wait_ge(S["gate_loaded"], 32)

            def turn_batch(b):
                pe.wait_ge(S["xnb_made"], b * 1 + 1)
                for k in range(BT):
                    ins = nc.tensor.transpose(trans_ps[:, k * C:(k + 1) * C], xnb[:, k, :], ident)
                    if k % 4 == 3:
                        ins.then_inc(S["trans_done"], 1)

            def norms(b, n):
                pe.wait_ge(S["squares_made"], b * 4 + (n + 3))
                nc.tensor.matmul(v_ps[32 * n:32 * n + 32, HALF:N], head_of, squares[:, n % 2, :], start=True, stop=True)\
                    .then_inc(S["norms_done"], 1)

            def project(b, last):
                pe.wait_ge(S["xnT_made_v"], b * 1 + 1)
                pe.wait_ge(S["xnT_made_a"], b * 1 + 1)
                for n in range(4):
                    u, m = n % 2, n // 2
                    pe.wait_ge(S["proj_read"], b * 4 + (n + 1))
                    for s in range(2):
                        ins = nc.tensor.matmul(proj_ps[u][:, s * HALF:(s + 1) * HALF], wT[:, 2 * u + s, :],
                                               xnT[:, m * HALF:(m + 1) * HALF], start=True, stop=True)
                    ins.then_inc(S["proj_done"], 1)
                    if n == 1:
                        pe.wait_ge(S["v_copied"], b + 1)
                        pe.wait_ge(S["gate_copied"], b + 1)
                        pe.wait_ge(S["norms_read"], b + 1)
                        for k in range(BT):
                            ins = nc.tensor.matmul(v_ps[:, k * C:(k + 1) * C], xnT[:, k * C:(k + 1) * C], wT[:, 4, :],
                                                   start=True, stop=True)
                        ins.then_inc(S["v_done"], 1)
                    if n >= 2:
                        if n == 2:
                            pe.wait_ge(S["v_copied"], b + 2)
                        norms(b, n - 2)
                for k in range(BT):
                    ins = nc.tensor.matmul(v_ps[:, k * E_:(k + 1) * E_], xnT[:, k * C:(k + 1) * C], gw_sb[:], start=True, stop=True)
                ins.then_inc(S["gate_done"], 1)
                if not last:
                    turn_batch(b + 1)
                norms(b, 2)
                norms(b, 3)

            turn_batch(0)
            with pe.Fori(0, B - 1) as b:
                project(b, False)
            project(B - 1, True)
            pe.wait_ge(S["bound_made"], 1)
            nc.tensor.matmul(trans_ps[0:1, HALF:HALF + P], bound[:], ident, start=True, stop=True).then_inc(S["bound_turned"], 1)
            def count_tokens():
                pe.wait_ge(S["masks_made"], 1)
                masks = rt[:, 8].rearrange("p k e -> p (k e)")
                nc.tensor.matmul(o_ps[1][:, 0:TILES * E_], before, masks, start=True, stop=True)
                nc.tensor.matmul(o_ps[1][:, TILES * E_:2 * TILES * E_], ones, masks, start=True, stop=True).then_inc(S["prefix_made"], 1)

            pe.wait_ge(S["v_copied"], B + 1)
            pe.wait_ge(S["gate_copied"], B + 1)
            pe.wait_ge(S["flag_made"], 1)

            def scores(t, j, first=False):
                half, mt = divmod(j, MT)
                if j == 0:
                    pe.wait_ge(S["ka_loaded"], t * (16 * QK_LOADS) + 16 * QK_LOADS)
                    pe.wait_ge(S["q0_loaded"], t * (16 * Q_LOADS) + 16 * Q_LOADS)
                if j == 4:
                    pe.wait_ge(S["kb_loaded"], t * (16 * QK_LOADS) + 16 * QK_LOADS)
                if j == MT:
                    pe.wait_ge(S["q1_loaded"], t * (16 * Q_LOADS) + 16 * Q_LOADS)
                for pair in range(2):
                    u = 2 * j + pair
                    if u >= SCORE_RING:
                        pe.wait_ge(S["exp_done"], t * UNITS + (u - SCORE_RING + 1))
                    elif not first and u < 2:
                        pe.wait_ge(S["exp_done"], t * UNITS - (1 - u))
                    for s in range(2):
                        ins = nc.tensor.matmul(score_ps[u % SCORE_RING][:, s * HALF:(s + 1) * HALF],
                                               k_st[:, mt * P:(mt + 1) * P],
                                               q_mv[:, 2 * pair + s, half * HALF:(half + 1) * HALF], start=True, stop=True)
                    ins.then_inc(S["scores_done"], 1)

            def values(t, j):
                half, mt = divmod(j, MT)
                pe.wait_ge(S["exp_done"], t * UNITS + (2 * j + 2))
                if j in (0, 4):
                    pe.wait_ge(S["v_loaded"], t * 2 + (j // 4 + 1))
                if mt == 0:
                    pe.wait_ge(S["o_free"], t * 2 + (half + 1))
                for h in range(HG):
                    ins = nc.tensor.matmul(o_ps[half][32 * h:32 * h + 32, :], v_st[:, mt, h, :],
                                           probs[:, j % PROB_RING, h, :], start=(mt == 0), stop=(mt == MT - 1))
                ins.then_inc(S["pv_done"], 1)

            def turn(t, half):
                pe.wait_ge(S["o_copied"], t * 2 + (half + 1))
                for k in range(4):
                    ins = nc.tensor.transpose(o_ps[half][:, k * P:(k + 1) * P], o_sb[:, half, k * P:(k + 1) * P], ident)
                ins.then_inc(S["o_turned"], 1)

            def step(t, first, last, count=False, experts_next=False, experts_before=False):
                for j in range(BLOCKS):
                    if j < BLOCKS - 1:
                        scores(t, j + 1)
                    elif not last:
                        scores(t + 1, 0)
                    elif experts_next:
                        pe.wait_ge(S["exp_done"], SPLIT * UNITS - 1)
                        turn_rows(0, 0)
                        turn_rows(1, 1)
                    if experts_before and j == 0:
                        pe.wait_ge(S["y_made"], SLOT_TILES + 2)
                    if count and j == MT:
                        pe.wait_ge(S["counts_read"], 2)
                    values(t, j)
                    if count and j == MT // 2:
                        count_tokens()
                    if j == 1 and not first:
                        turn(t - 1, 1)
                    if j == MT + 2:
                        turn(t, 0)
            with pe.If(pe.value_load(flag_i[0:1, 0:1], min_val=0, max_val=1)):
                with pe.Fori(0, STEPS) as t:
                    pe.wait_ge(S["mx_loaded"], t * (16 * 30) + 16 * 30)
                    for h in range(HG):
                        for nt in range(MT):
                            n = h * MT + nt
                            pe.wait_ge(S["mx_read"], t * (HG * MT) + (n + 1))
                            for s in range(2):
                                ins = nc.tensor.matmul(score_ps[n % 2][:, s * HALF:(s + 1) * HALF], q_mv[:, h, nt * P:(nt + 1) * P],
                                                       k_st[:, s * HALF:(s + 1) * HALF], start=True, stop=True)
                            ins.then_inc(S["mx_scores"], 1)
                    pe.wait_ge(S["mx_made"], t * 3 + 3)
                    nc.tensor.transpose(score_ps[2][:, 0:P], shift_nt[:].rearrange("p m a h -> p (m a h)"), ident)\
                        .then_inc(S["mx_turned"], 1)
                pe.wait_ge(S["mx_read"], STEPS * HG * MT + 2)
                pe.wait_ge(S["mx_copied"], STEPS)
                pe.wait_ge(S["mx_loaded"], 16 * (30 * (STEPS + 1) + 2))

            def in_count(j, par):
                return (j - par) * 8 + 16

            def turn_rows(j, par):
                pe.wait_ge(xs_in[par], in_count(j, par))
                for k in range(2):
                    ins = nc.tensor.transpose(xs_ps[par][:, k * P:(k + 1) * P], xs_sb[:, par, k, :], ident)
                ins.then_inc(S["xs_turned"], 1)

            def layer1(j, par):
                pe.wait_ge(w1_in[par], in_count(j, par))
                pe.wait_ge(S["xsT_made"], j + 1)
                for m in range(2):
                    nc.tensor.matmul(h1_ps[m][:, 0:ST], w1_sb[:, par, m * P:(m + 1) * P],
                                     xsT[:, par, :], start=True, stop=True).then_inc(S["l1_done"], 1)

            def layer2(j, par):
                pe.wait_ge(w2_in[par], in_count(j, par))
                pe.wait_ge(S["g1_done"], j + 1)
                for m in range(2):
                    for k in range(2):
                        ins = nc.tensor.matmul(h2_ps[m][:, 0:ST], w2_sb[:, par, k, m * P:(m + 1) * P],
                                               h1[:, par, k, :], start=(k == 0), stop=(k == 1))
                    ins.then_inc(S["l2_done"], 1)

            def layer3(j, par):
                pe.wait_ge(w3_in[par], in_count(j, par))
                pe.wait_ge(S["g2_done"], j + 1)
                pe.wait_ge(S["y_made"], j + 1)
                for m in range(2):
                    for k in range(2):
                        ins = nc.tensor.matmul(y_ps[par][:, m * C:(m + 1) * C], h2[:, par, k, m * P:(m + 1) * P],
                                               w3_sb[:, par, k, :], start=(k == 0), stop=(k == 1))
                ins.then_inc(S["l3_done"], 1)

            scores(0, 0, first=True)
            step(0, True, False, count=True)
            with pe.Fori(1, SPLIT - 1) as t:
                step(t, False, False)
            step(SPLIT - 1, False, True, experts_next=True)

            layer1(0, 0)
            turn(SPLIT - 1, 1)
            layer2(0, 0)
            pe.wait_ge(S["o_free"], 2 * SPLIT + 2)
            with pe.Fori(0, (SLOT_TILES - 1) // 2) as i:
                for k in range(2):
                    layer1(i * 2 + (1 + k), 1 - k)
                    turn_rows(i * 2 + (2 + k), k)
                    layer3(i * 2 + k, k)
                    layer2(i * 2 + (1 + k), 1 - k)
            pe.wait_ge(S["xsT_made"], SLOT_ROOM)
            pe.wait_ge(S["g1_done"], SLOT_TILES)
            scores(SPLIT, 0, first=True)
            layer3(SLOT_TILES - 1, 0)

            step(SPLIT, True, False, experts_before=True)
            with pe.Fori(SPLIT + 1, STEPS - 1) as t:
                step(t, False, False)
            step(STEPS - 1, False, True)
            turn(STEPS - 1, 1)


_INS = ['L0_attn_x', 'L0_attn_Wq', 'L0_attn_Wk', 'L0_attn_Wv', 'L0_ffn_w1', 'L0_ffn_b1', 'L0_ffn_w2', 'L0_ffn_b2',
        'L0_ffn_w3', 'L0_ffn_b3', 'L0_ffn_gate_w', 'L0_ffn_gate_b']


def _constants():
    import numpy as np
    d = np.arange(C) % D
    inv = np.power(np.float32(10000.0), (np.float32(-2.0) * np.arange(D // 2, dtype=np.float32) / np.float32(D)).astype(np.float32))
    ang = (np.arange(N, dtype=np.float32)[:, None] * inv.astype(np.float32)[None, :]).astype(np.float32)
    cos, sin = np.cos(ang).astype(np.float32), np.sin(ang).astype(np.float32)
    rope_cos = np.ascontiguousarray(cos[:, d // 2].T)
    rope_sin = np.ascontiguousarray(sin[:, d // 2].T * np.where(d % 2, 1, -1).astype(np.float32)[:, None])
    consts = np.zeros((P, 3 * P + 8 + 40 + 32 + 32), np.float32)
    consts[:, 0:P] = np.eye(P)
    consts[:, P:2 * P] = np.arange(P)[:, None] < np.arange(P)[None, :]
    consts[:, 2 * P:3 * P] = 1
    consts[:, 384:392] = E_ - np.arange(E_)
    consts[:, 392:432] = np.arange(40)
    consts[:, 432:464] = ST * np.arange(32)
    consts[:, 464:480] = np.arange(P)[:, None] // D == np.arange(H)[None, :]
    return rope_cos, rope_sin, consts


def kernel(**inputs):
    import numpy as _np
    import concourse.bacc as _bacc
    from concourse import mybir as _mybir
    from concourse.bass_utils import run_bass_kernel_spmd as _run

    nc = _bacc.Bacc("TRN2", target_bir_lowering=False, num_devices=1)
    arrays, args = {}, []
    for name in _INS:
        a = _np.ascontiguousarray(inputs[name])
        arrays[f"in_{name}_dram"] = a
        args.append(nc.dram_tensor(f"in_{name}_dram", a.shape, _mybir.dt.from_np(a.dtype), kind="ExternalInput").ap())
    for name, a in zip(("rope_cos", "rope_sin", "consts"), _constants()):
        arrays[f"in_{name}_dram"] = a
        args.append(nc.dram_tensor(f"in_{name}_dram", a.shape, _mybir.dt.from_np(a.dtype), kind="ExternalInput").ap())
    args.append(nc.dram_tensor("out_0_dram", (B, N, C), F32, kind="ExternalOutput").ap())
    build(nc, *args)
    r = _run(nc, [arrays], core_ids=[0])
    return r.results[0]["out_0_dram"]
```
